# Optimizing a Trainium2 kernel written in Bass

```python
import numpy as np
import jax
import jax.numpy as jnp

def _softmax(x, axis=-1):
    return jax.nn.softmax(x, axis=axis)

def _gelu(x):
    return jax.nn.gelu(x, approximate=True)

def _silu(x):
    return jax.nn.silu(x)

def _sigmoid(x):
    return jax.nn.sigmoid(x)

def _layernorm(x, axis=-1, eps=1e-05):
    m = jnp.mean(x, axis=axis, keepdims=True)
    v = jnp.var(x, axis=axis, keepdims=True)
    return (x - m) / jnp.sqrt(v + eps)

def _scatter_add(tgt, idx, src, axis=0):
    return tgt.at[idx].add(src)

def _segment_sum(src, seg, n):
    return jax.ops.segment_sum(src, seg, n)
kernel_name = 'mk_recurrent_d1_jaxref_r4_6f8e87'

def setup_inputs(seed: int=0):
    np.random.seed(seed)
    _w = jnp.asarray

    def _L0_attn_setup():
        import jax, jax.numpy as jnp
        import numpy as np
        B, N, H = (1, 1024, 512)
        NH, HD = (16, H // 16)
        WINDOW = 1024
        EPS = 1e-06
        THETA = 10000.0
        NEG = -1e+30

        def rmsnorm(x, w):
            var = jnp.mean(jnp.square(x.astype(jnp.float32)), axis=-1, keepdims=True)
            return (x * jax.lax.rsqrt(var + EPS)).astype(w.dtype) * w

        def rotate_half(x):
            x1, x2 = (x[..., :x.shape[-1] // 2], x[..., x.shape[-1] // 2:])
            return jnp.concatenate((-x2, x1), axis=-1)
        key = jax.random.key(seed)
        k1, k2, k3 = jax.random.split(key, 3)
        x = jax.random.normal(k1, (B, N, H), dtype=jnp.float32)
        w_qkv = jax.random.normal(k2, (H, 3 * H), dtype=jnp.float32) * (1.0 / np.sqrt(H))
        w_out = jax.random.normal(k3, (H, H), dtype=jnp.float32) * (1.0 / np.sqrt(H))
        q_gamma = jnp.ones((HD,), dtype=jnp.float32)
        k_gamma = jnp.ones((HD,), dtype=jnp.float32)
        return {'x': x, 'w_qkv': w_qkv, 'w_out': w_out, 'q_gamma': q_gamma, 'k_gamma': k_gamma}
    _L0_attn_in = _L0_attn_setup()

    def _L0_ffn_setup():
        import jax, jax.numpy as jnp
        import numpy as np
        DIM = 512
        HID = 1408
        ZERO_POINT = 128.0

        def _qlinear(x, wq, scale):
            W = (wq.astype(jnp.float32) - ZERO_POINT) * scale[:, None]
            return jnp.einsum('bsd,hd->bsh', x, W)
        key = jax.random.key(seed)
        ks = jax.random.split(key, 7)
        B, S = (4, 512)
        sg = jax.random.uniform(ks[1], (HID,)) * (0.02 / np.sqrt(DIM)) + 0.0001
        su = jax.random.uniform(ks[3], (HID,)) * (0.02 / np.sqrt(DIM)) + 0.0001
        sd = jax.random.uniform(ks[5], (DIM,)) * (0.02 / np.sqrt(HID)) + 0.0001
        return {'x': jax.random.normal(ks[0], (B, S, DIM), dtype=jnp.float32), 'wq_gate': jax.random.randint(ks[2], (HID, DIM), 0, 64, dtype=jnp.int32), 's_gate': sg, 'wq_up': jax.random.randint(ks[4], (HID, DIM), 0, 64, dtype=jnp.int32), 's_up': su, 'wq_down': jax.random.randint(ks[6], (DIM, HID), 0, 64, dtype=jnp.int32), 's_down': sd}
    _L0_ffn_in = _L0_ffn_setup()
    _d = {'L0_attn_x': _L0_attn_in['x'], 'L0_attn_w_qkv': _L0_attn_in['w_qkv'], 'L0_attn_w_out': _L0_attn_in['w_out'], 'L0_attn_q_gamma': _L0_attn_in['q_gamma'], 'L0_attn_k_gamma': _L0_attn_in['k_gamma'], 'L0_ffn_wq_gate': _L0_ffn_in['wq_gate'], 'L0_ffn_s_gate': _L0_ffn_in['s_gate'], 'L0_ffn_wq_up': _L0_ffn_in['wq_up'], 'L0_ffn_s_up': _L0_ffn_in['s_up'], 'L0_ffn_wq_down': _L0_ffn_in['wq_down'], 'L0_ffn_s_down': _L0_ffn_in['s_down']}
    _x0 = _d['L0_attn_x']
    _d['L0_attn_x'] = jax.random.normal(jax.random.fold_in(jax.random.key(seed), 1), (4, 512, 512), dtype=_x0.dtype)
    del _x0
    return _d

def reference(L0_attn_x, L0_attn_w_qkv, L0_attn_w_out, L0_attn_q_gamma, L0_attn_k_gamma, L0_ffn_wq_gate, L0_ffn_s_gate, L0_ffn_wq_up, L0_ffn_s_up, L0_ffn_wq_down, L0_ffn_s_down):

    def _L0_attn_ref(x, w_qkv, w_out, q_gamma, k_gamma):
        import jax, jax.numpy as jnp
        import numpy as np
        B, N, H = (1, 1024, 512)
        NH, HD = (16, H // 16)
        WINDOW = 1024
        EPS = 1e-06
        THETA = 10000.0
        NEG = -1e+30

        def rmsnorm(x, w):
            var = jnp.mean(jnp.square(x.astype(jnp.float32)), axis=-1, keepdims=True)
            return (x * jax.lax.rsqrt(var + EPS)).astype(w.dtype) * w

        def rotate_half(x):
            x1, x2 = (x[..., :x.shape[-1] // 2], x[..., x.shape[-1] // 2:])
            return jnp.concatenate((-x2, x1), axis=-1)
        b, n, _ = x.shape
        qkv = jnp.einsum('bnh,hm->bnm', x, w_qkv)
        q, k, v = jnp.split(qkv, 3, axis=-1)
        q = q.reshape(b, n, NH, HD).transpose(0, 2, 1, 3)
        k = k.reshape(b, n, NH, HD).transpose(0, 2, 1, 3)
        v = v.reshape(b, n, NH, HD).transpose(0, 2, 1, 3)
        q = rmsnorm(q, q_gamma)
        k = rmsnorm(k, k_gamma)
        inv_freq = 1.0 / THETA ** (jnp.arange(0, HD, 2, dtype=jnp.float32) / HD)
        t = jnp.arange(n, dtype=jnp.float32)
        freqs = t[:, None] * inv_freq[None, :]
        emb = jnp.concatenate((freqs, freqs), axis=-1)
        cos = jnp.cos(emb)[None, None, :, :]
        sin = jnp.sin(emb)[None, None, :, :]
        q = q * cos + rotate_half(q) * sin
        k = k * cos + rotate_half(k) * sin
        kv_len = k.shape[-2]
        q_idx = jnp.arange(n)[:, None] + (kv_len - n)
        k_idx = jnp.arange(kv_len)[None, :]
        mask = (q_idx >= k_idx) & (q_idx - k_idx <= WINDOW)
        scores = jnp.einsum('bhqd,bhkd->bhqk', q, k) / np.sqrt(HD)
        scores = jnp.where(mask[None, None, :, :], scores, NEG)
        attn = jax.nn.softmax(scores, axis=-1)
        out = jnp.einsum('bhqk,bhkd->bhqd', attn, v)
        out = out.transpose(0, 2, 1, 3).reshape(b, n, H)
        return jnp.einsum('bnh,hm->bnm', out, w_out)

    def _L0_ffn_ref(x, wq_gate, s_gate, wq_up, s_up, wq_down, s_down):
        import jax, jax.numpy as jnp
        import numpy as np
        DIM = 512
        HID = 1408
        ZERO_POINT = 128.0

        def _qlinear(x, wq, scale):
            W = (wq.astype(jnp.float32) - ZERO_POINT) * scale[:, None]
            return jnp.einsum('bsd,hd->bsh', x, W)
        gate = _qlinear(x, wq_gate, s_gate)
        gate = jax.nn.silu(gate)
        up = _qlinear(x, wq_up, s_up)
        return _qlinear(gate * up, wq_down, s_down)
    x = L0_attn_x
    xn = _layernorm(x, axis=-1)
    s = _L0_attn_ref(xn, L0_attn_w_qkv, L0_attn_w_out, L0_attn_q_gamma, L0_attn_k_gamma)
    g = _silu(_L0_ffn_ref(xn, L0_ffn_wq_gate, L0_ffn_s_gate, L0_ffn_wq_up, L0_ffn_s_up, L0_ffn_wq_down, L0_ffn_s_down))
    x = x + s * g
    return x

_drawn_inputs = setup_inputs


def setup_inputs(seed=0):
    import zlib

    import numpy as np

    out = dict(_drawn_inputs(seed))
    spreads = {'L0_attn_q_gamma': (1.0, 0.6), 'L0_attn_k_gamma': (1.0, 0.6)}
    factors = {'L0_attn_w_qkv': 8.0,
     'L0_attn_w_out': 8.0,
     'L0_ffn_s_gate': 8.0,
     'L0_ffn_s_up': 8.0,
     'L0_ffn_s_down': 8.0}
    for name, (base, spread) in spreads.items():
        noise = np.random.default_rng([zlib.crc32(name.encode()), seed]).standard_normal(out[name].shape)
        drawn = base * np.exp(spread * noise) if base else spread * noise
        out[name] = jnp.asarray(drawn.astype(out[name].dtype))
    for name, factor in factors.items():
        out[name] = (out[name] * factor).astype(out[name].dtype)
    return out
```

```python
from contextlib import ExitStack

import numpy as np

import concourse.bass as bass
from concourse import mybir

ALU = mybir.AluOpType
ACT = mybir.ActivationFunctionType
AX = mybir.AxisListType
F32 = mybir.dt.float32
F32R = mybir.dt.float32r
BF16 = mybir.dt.bfloat16
I32 = mybir.dt.int32

B, N, H = 4, 512, 512
NH = 16
HD = H // NH
P = 128
TB = N // P
KT = H // P
G = 4
HG = NH // G
GC = HG * HD
HID = 1408
MT = HID // P
LN_EPS, RMS_EPS, THETA, NEG, ZERO = 1e-5, 1e-6, 10000.0, -1e30, 128.0
SCALE = 1.0 / float(np.sqrt(HD))
VW = 2 * HD + 1
KS = 3 * HD
NP_ = 4
ST_OPS = [[(0, 0, 512)], [(1, 0, 384), (3, 384, 128)], [(2, 0, 256)]]
SM_OPS = [[(3, 0, 512)], [(2, 0, 384), (0, 384, 128)], [(1, 0, 256)]]
NOP = len(ST_OPS)
UO = HG * NOP


def wait(eng, sem, value):
    if isinstance(value, int) and value <= 0:
        return
    eng.wait_ge(sem, value)


def wait_slot(eng, sem, n, pos, ring=2):
    value = n - pos if pos < ring - 1 else n - ring + 1
    if isinstance(value, int) and value <= 0:
        return
    eng.wait_ge(sem, value)


def build(nc, x, w_qkv, w_out, q_gamma, k_gamma, w_gate, s_gate, w_up, s_up, w_down, s_down,
          cos_tab, sin_tab, ident, ident_b, mask_s, mask_t, s_dram, rd_dram, xnt_dram, out):
    top = ExitStack()
    with top:
        def sem(name):
            return top.enter_context(nc.semaphore(name))

        def tiles(stack):
            def sb(name, shape, dt=F32):
                return stack.enter_context(nc.sbuf_tensor(name, shape, dt))
            return sb

        psum = [top.enter_context(nc.psum_tensor(f"bank{n}", [P, 512], F32)) for n in range(8)]
        QKV_PS, X_PS, W_PS, ST_PS, PV_PS = psum[0:2], psum[2:4], psum[4], psum[5:7], psum[7]
        GU_PS, DN_PS = psum[0:4], psum[4:8]

        pa = ExitStack()
        sb = tiles(pa)
        wq_h = sb("wq_h", [P, KT, G * 3 * GC], F32R)
        wq_l = sb("wq_l", [P, KT, G * 3 * GC], F32R)
        wo_h = sb("wo_h", [P, KT, H], F32R)
        wo_l = sb("wo_l", [P, KT, H], F32R)
        xnt_h = sb("xnt_h", [P, KT, N], F32R)
        xnt_l = sb("xnt_l", [P, KT, N], F32R)
        idf = sb("idf", [P, P])
        idr = sb("idr", [P, P], F32R)
        idb = sb("idb", [P, P], BF16)
        msk_s = sb("msk_s", [P, P], BF16)
        msk_t = sb("msk_t", [P, P], BF16)
        ctab = sb("ctab", [P, TB, HD])
        stab = sb("stab", [P, TB, HD])
        gam = sb("gam", [P, 2, HD])
        cg = sb("cg", [P, TB, 2, HD])
        sg = sb("sg", [P, TB, 2, HD])
        half = sb("half", [P, 8])
        xr = sb("xr", [P, TB, H])
        st6 = sb("st6", [P, 2, 8])
        mv = sb("mv", [P, 2, 8])
        ve = sb("ve", [P, 2, 8])
        rstd = sb("rstd", [P, 2, 8])
        sq = sb("sq", [P, 2, 2 * HG, HD + 1])
        ss = sb("ss", [P, 2, 8])
        rr = sb("rr", [P, 2, 8])
        qn = sb("qn", [P, 2, 2, HG, HD])
        ra = sb("ra", [P, 2, 2, HG, HD])
        rb = sb("rb", [P, 2, 2, HG, HD])
        qp = sb("qp", [P, 2, 2 * GC])
        tt = sb("tt", [P, 2, HG, 6, HD], F32R)
        qst = sb("qst", [P, 2, HG, N], F32R)
        kst = sb("kst", [P, 2, HG, N], F32R)
        va = sb("va", [P, 2, TB, HG, VW], F32R)
        mx = sb("mx", [P, HG * TB])
        mrow = sb("mrow", [HG * TB, P], F32R)
        den16 = sb("den16", [P, HG * TB])
        rd16 = sb("rd16", [P, HG * TB])
        with ExitStack() as early:
            stage = tiles(early)("stage", [P, KT, G * 3 * GC + H])
        pf = sb("pf", [P, NP_, 512])
        ph = sb("ph", [P, NP_, 512], F32R)
        pl = sb("pl", [P, NP_, 512], F32R)
        oraw = sb("oraw", [VW, HG, N])
        oh = sb("oh", [P, N])
        ol = sb("ol", [P, N])
        rdb = sb("rdb", [P, N])
        on = sb("on", [P, N])
        on_h = sb("on_h", [P, G, N], F32R)
        on_l = sb("on_l", [P, G, N], F32R)
        s_sb = xr
        pa.close()

        pbs = ExitStack()
        sb = tiles(pbs)
        wgu = sb("wgu", [P, MT, KT, 2 * P], F32R)
        wd = sb("wd", [P, MT, H], F32R)
        xb_h = sb("xb_h", [P, 2, KT, N], F32R)
        xb_l = sb("xb_l", [P, 2, KT, N], F32R)
        ht_h = sb("ht_h", [P, MT, N], F32R)
        ht_l = sb("ht_l", [P, MT, N], F32R)
        wst = sb("wst", [P, 2, KT * 2 * P], I32)
        sgu = sb("sgu", [P, 2, MT])
        sdb = sb("sdb", [P, H])
        gs = sb("gs", [P, 2, N])
        hf = sb("hf", [P, 2, N])
        yt = sb("yt", [P, 2, H])
        gt = sb("gt", [P, 2, H])
        xs = sb("xs", [P, 2, 2, H])
        res = sb("res", [P, 2, H])
        pbs.close()

        c_in = sem("c_in")
        w_in = [sem(f"w_in{g}") for g in range(G + 1)]
        w_hi, w_lo = sem("w_hi"), sem("w_lo")
        idr_ok, ones_ok, tab_c, tab_ok = sem("idr_ok"), sem("ones_ok"), sem("tab_c"), sem("tab_ok")
        x_in = [sem(f"x_in{t}") for t in range(TB)]
        ln_s, ln_a, ln_v, ln_r = sem("ln_s"), sem("ln_a"), sem("ln_v"), sem("ln_r")
        xn_ok, xt_full, xt_hi, xt_lo = sem("xn_ok"), sem("xt_full"), sem("xt_hi"), sem("xt_lo")
        xs_out = sem("xs_out")
        qkv_full, sq_ok, vh_ok, ss_ok, rr_ok = (sem(n) for n in ("qkv_full", "sq_ok", "vh_ok", "ss_ok", "rr_ok"))
        qn_ok, vl_ok, rope_ok, qp_ok = (sem(n) for n in ("qn_ok", "vl_ok", "rope_ok", "qp_ok"))
        th_ok, tl_ok, tq_full, tk_full = (sem(n) for n in ("th_ok", "tl_ok", "tq_full", "tk_full"))
        tq_ev, tk_ev = sem("tq_ev"), sem("tk_ev")
        sm_full, sm_ok, mt_full, mt_ok, m_in = (sem(n) for n in ("sm_full", "sm_ok", "mt_full", "mt_ok", "m_in"))
        st_full, p_ok, pl_ok, pv_ok, o_ev = (sem(n) for n in ("st_full", "p_ok", "pl_ok", "pv_ok", "o_ev"))
        og_in, d_in, rd_ok, rd_out, rb_in = (sem(n) for n in ("og_in", "d_in", "rd_ok", "rd_out", "rb_in"))
        os_ok, on_ok, onh_ok, onl_ok = (sem(n) for n in ("os_ok", "on_ok", "onh_ok", "onl_ok"))
        wo_full, s_ev = sem("wo_full"), sem("s_ev")
        s_out = [sem("s_out0"), sem("s_out1")]
        a_act, a_dve, a_pool = sem("a_act"), sem("a_dve"), sem("a_pool")
        ws_in = [sem("ws_in0"), sem("ws_in1")]
        wc_ok, wd_ok, c2_in = sem("wc_ok"), sem("wd_ok"), sem("c2_in")
        xb_in = [sem("xb_in0"), sem("xb_in1")]
        gu_full, gs_ok, hf_ok, hh_ok, hl_ok = (sem(n) for n in ("gu_full", "gs_ok", "hf_ok", "hh_ok", "hl_ok"))
        dn_full, y_ok, g_ok, sgx_ok, res_ok = (sem(n) for n in ("dn_full", "y_ok", "g_ok", "sgx_ok", "res_ok"))
        xs_in = [sem("xs_in0"), sem("xs_in1")]
        r_out = [sem("r_out0"), sem("r_out1")]

        block = top.enter_context(nc.Block())

        def run_slots(eng, slot):
            slot(-1, 3)
            slot(0, 0)
            with eng.Fori(0, B - 1) as b:
                for c in range(1, 5):
                    slot(b, c)
            for c in range(1, 4):
                slot(B - 1, c)

        def parts(b, c):
            i = 4 * b + c
            return i, c % 2, i + 1, (c + 1) % 2, b + (c + 1) // 4, (c + 1) % 4

        def last(b, c):
            return isinstance(b, int) and 4 * b + c == 4 * B - 1

        def ln_slot(b, c):
            return c == 2 and not (isinstance(b, int) and b == B - 1)

        @block.sync
        def _(sp):
            def load_x(b, t):
                sp.dma_start(xr[:, t, :], x[b, t * P:(t + 1) * P, :]
                             if isinstance(b, int) else
                             x[bass.ds(b, 1), t * P:(t + 1) * P, :].rearrange("o p d -> (o p) d")
                             ).then_inc(x_in[t], 16)

            load_x(0, 0)
            load_x(0, 1)
            sp.dma_start(idf[:], ident).then_inc(c_in, 16)
            sp.dma_start(stage[:, :, 0:3 * GC], w_qkv[:, :, 0:3 * GC]).then_inc(w_in[0], 16)
            load_x(0, 2)
            load_x(0, 3)
            for g in range(1, G):
                sp.dma_start(stage[:, :, g * 3 * GC:(g + 1) * 3 * GC],
                             w_qkv[:, :, g * 3 * GC:(g + 1) * 3 * GC]).then_inc(w_in[g], 16)
            sp.dma_start(stage[:, :, G * 3 * GC:], w_out).then_inc(w_in[G], 16)

            def gather(b, c, h):
                i = 4 * b + c
                wait(sp, o_ev, 4 * i + h + 1)
                wait(sp, os_ok, i)
                sp.dma_start(oh[HD * h:HD * h + HD, :], oraw[0:HD, h, :]).then_inc(og_in, 16)
                sp.dma_start(ol[HD * h:HD * h + HD, :], oraw[HD:2 * HD, h, :]).then_inc(og_in, 16)

            def den_out(b, c):
                i = 4 * b + c
                wait(sp, rd_ok, i)
                sp.dma_start(den16[:], oraw[2 * HD:VW, :, :].rearrange("o h (a n) -> o (h a) n", n=HG * TB)
                             ).then_inc(d_in, 16)

            def den_in(b, c):
                i = 4 * b + c
                wait(sp, rd_ok, i + 1)
                sp.dma_start(rd_dram[0:1, :].rearrange("o (p n) -> (o p) n", n=HG * TB),
                             rd16[:]).then_inc(rd_out, 16)
                wait(sp, rd_out, 16 * (i + 1))
                wait(sp, on_ok, i)
                sp.dma_start(rdb[:], rd_dram.rearrange("o (h n) -> (o h) n", h=HG).rearrange(
                    "h (o n) -> h o n", o=1).to_broadcast([HG, HD, N])).then_inc(rb_in, 16)

            def slot(b, c):
                i, par, i1, par1, b1, g1 = parts(b, c)
                attend = not (isinstance(i, int) and i < 0)
                if c == 1 and not (isinstance(b, int) and b == B - 1):
                    stored, turned = sp.snap(32 * b), sp.snap(4 * (b + 1))
                    wait(sp, s_out[0], stored)
                    wait(sp, s_out[1], stored)
                    wait(sp, xt_full, turned)
                    for t in range(TB):
                        load_x(b + 1, t)
                if attend:
                    for h in range(HG):
                        gather(b, c, h)
                    den_out(b, c)
                    den_in(b, c)
                if c == 4 or (isinstance(i, int) and i == 0):
                    nb = b + 1 if c == 4 else 0
                    wait(sp, xt_hi, 4 * nb + 4)
                    wait(sp, xt_lo, 4 * nb + 4)
                    for n, t in ((0, xnt_h), (1, xnt_l)):
                        dst = xnt_dram[n, nb] if isinstance(nb, int) else \
                            xnt_dram[n, bass.ds(nb, 1)].rearrange("o p k n -> (o p) k n")
                        sp.dma_start(dst, t[:].bitcast(F32)).then_inc(xs_out, 16)

            run_slots(sp, slot)
            sp.wait_ge(a_act, 1)
            sp.wait_ge(a_dve, 1)
            sp.wait_ge(a_pool, 1)
            sp.wait_ge(wo_full, 4 * B)
            sp.wait_ge(s_out[0], 16 * 2 * B)
            sp.wait_ge(s_out[1], 16 * 2 * B)
            sp.wait_ge(xs_out, 32 * B)

            def load_xb(b, par):
                for n, t in ((0, xb_h), (1, xb_l)):
                    src = xnt_dram[n, b] if isinstance(b, int) else \
                        xnt_dram[n, bass.ds(b, 1)].rearrange("o p k n -> (o p) k n")
                    sp.dma_start(t[:, par].bitcast(F32), src).then_inc(xb_in[par], 16)

            load_xb(0, 0)
            for m in range(MT):
                if m >= 2:
                    sp.wait_ge(wc_ok, m - 1)
                sp.dma_start(wst[:, m % 2, :], w_gate[m].rearrange("p k n -> p (k n)")).then_inc(ws_in[m % 2], 16)
                if m == 0:
                    sp.dma_start(sgu[:, 0, :], s_gate).then_inc(c2_in, 16)
                    sp.dma_start(sgu[:, 1, :], s_up).then_inc(c2_in, 16)
                    sp.dma_start(sdb[:], s_down.to_broadcast([P, H])).then_inc(c2_in, 16)
            for q in range(MT):
                n = MT + q
                sp.wait_ge(wc_ok, n - 1)
                sp.dma_start(wst[:, n % 2, 0:H], w_down[q]).then_inc(ws_in[n % 2], 16)

            def load_xs(b, t):
                n = 4 * b + t
                wait_slot(sp, res_ok, n, t)
                rows = slice(t * P, (t + 1) * P)
                for a, src in ((0, x), (1, s_dram)):
                    v = src[b, rows, :] if isinstance(b, int) else \
                        src[bass.ds(b, 1), rows, :].rearrange("o p d -> (o p) d")
                    sp.dma_start(xs[:, t % 2, a, :], v).then_inc(xs_in[t % 2], 16)

            def store(b, t):
                n = 4 * b + t
                wait(sp, res_ok, n + 1)
                v = out[bass.ds(b, 1), t * P:(t + 1) * P, :].rearrange("o p d -> (o p) d")
                sp.dma_start(v, res[:, t % 2, :]).then_inc(r_out[t % 2], 16)

            with sp.Fori(0, B // 2) as bb:
                for e in range(2):
                    b = 2 * bb + e
                    if e == 0:
                        wait(sp, gu_full, MT * (2 * bb))
                        load_xb(b + 1, 1)
                    else:
                        wait(sp, gu_full, MT * (2 * bb + 1))
                        load_xb(2, 0)
                    for t in range(TB):
                        load_xs(b, t)
                        if t >= 1:
                            store(b, t - 1)
                    store(b, TB - 1)
            for n in range(2):
                sp.wait_ge(r_out[n], 16 * 2 * B)
                sp.wait_ge(xb_in[n], 32 * (B // 2 + (n == 0)))

        @block.gpsimd
        def _(pool):
            pool.memset(kst[KS:KS + 1, :, :, :].bitcast(F32), 1.0).then_inc(ones_ok, 1)
            pool.wait_ge(ones_ok, 1)
            pool.memset(half[:], -0.5).then_inc(ones_ok, 1)
            pool.memset(sq[:, :, :, HD:HD + 1], HD * RMS_EPS).then_inc(ones_ok, 1)
            pool.memset(va[:, :, :, :, 2 * HD:VW].bitcast(F32), 1.0).then_inc(ones_ok, 1)
            pool.wait_ge(c_in, 16 * 8)
            for a in range(2):
                for t in range(TB):
                    pool.tensor_tensor(cg[:, t, a, :], ctab[:, t, :], gam[:, a, :], ALU.mult).then_inc(tab_ok, 1)
                    for lo, hi in ((0, HD // 2), (HD // 2, 0)):
                        pool.tensor_tensor(sg[:, t, a, lo:lo + HD // 2], stab[:, t, lo:lo + HD // 2],
                                           gam[:, a, hi:hi + HD // 2], ALU.mult).then_inc(tab_ok, 1)
            pool.wait_ge(tab_ok, 2 * TB * 3)

            def rstd_block(b, t):
                n = 4 * b + t
                wait(pool, ln_v, n + 1)
                pool.tensor_tensor(rstd[:, t % 2, 0:1], ve[:, t % 2, 0:1], half[:, 0:1], ALU.pow).then_inc(ln_r, 1)

            def rope(i, t):
                n = 4 * i + t
                s = t % 2
                wait(pool, ss_ok, n + 1)
                pool.tensor_tensor(rr[:, s, :], ss[:, s, :], half[:], ALU.pow).then_inc(rr_ok, 1)
                wait(pool, qn_ok, n + 1)
                wait(pool, qp_ok, n - 1)
                hh = HD // 2
                for a in range(2):
                    pool.tensor_tensor(ra[:, s, a], qn[:, s, a],
                                       cg[:, t, a, :].rearrange("p (o d) -> p o d", o=1).to_broadcast([P, HG, HD]), ALU.mult)
                for a in range(2):
                    for lo, hi in ((0, hh), (hh, 0)):
                        op = pool.tensor_tensor(
                            rb[:, s, a, :, lo:lo + hh], qn[:, s, a, :, hi:hi + hh],
                            sg[:, t, a, lo:lo + hh].rearrange("p (o d) -> p o d", o=1).to_broadcast([P, HG, hh]), ALU.mult)
                op.then_inc(rope_ok, 1)

            def norm(b, c):
                i = 4 * b + c
                wait(pool, og_in, 16 * 2 * HG * (i + 1))
                wait(pool, onl_ok, i)
                pool.tensor_tensor(on[:], oh[:], ol[:], ALU.add).then_inc(os_ok, 1)
                wait(pool, os_ok, i + 1)
                wait(pool, rb_in, 16 * (i + 1))
                pool.tensor_tensor(on[:], on[:], rdb[:], ALU.mult).then_inc(on_ok, 1)

            def slot(b, c):
                i, par, i1, par1, b1, g1 = parts(b, c)
                for k in range(TB):
                    if isinstance(i, int) and i < 0 and k < 2:
                        rstd_block(0, k + 2)
                    if not last(b, c):
                        rope(i1, k)
                    if ln_slot(b, c):
                        rstd_block(b + 1, k)
                    if k == 2 and not (isinstance(i, int) and i < 1):
                        norm(b, c - 1)

            rstd_block(0, 0)
            rstd_block(0, 1)
            run_slots(pool, slot)
            norm(B - 1, 3)
            pool.sem_inc(a_pool, 1)

        @block.scalar
        def _(act):
            for dst, src in ((idb[:], ident_b), (msk_s[:], mask_s), (msk_t[:], mask_t), (ctab[:], cos_tab),
                             (stab[:], sin_tab), (gam[:, 0, :], q_gamma.to_broadcast([P, HD])),
                             (gam[:, 1, :], k_gamma.to_broadcast([P, HD]))):
                act.dma_start(dst, src).then_inc(c_in, 16)

            def split_w(g):
                act.wait_ge(w_in[g], 16)
                if g < G:
                    cols = slice(g * 3 * GC, (g + 1) * 3 * GC)
                    act.activation(wq_h[:, :, cols], stage[:, :, cols], ACT.Copy).then_inc(w_hi, 1)
                else:
                    act.activation(wo_h[:], stage[:, :, G * 3 * GC:], ACT.Copy).then_inc(w_hi, 1)

            def xt_high(b, t):
                n = 4 * b + t
                wait(act, xt_full, n + 1)
                if t == 0:
                    wait(act, xs_out, 32 * b)
                wait(act, qkv_full, 4 * (4 * b - 1) + t + 1)
                act.activation(xnt_h[:, :, t * P:(t + 1) * P], W_PS[:].rearrange("p (k n) -> p k n", k=KT),
                               ACT.Copy).then_inc(xt_hi, 1)

            def square(i, par, t):
                n = 4 * i + t
                s = t % 2
                wait(act, qkv_full, n + 1)
                wait(act, ss_ok, n - 1)
                act.activation(sq[:, s, :, 0:HD], QKV_PS[s][:, 0:2 * GC].rearrange("p (h d) -> p h d", d=HD),
                               ACT.Square).then_inc(sq_ok, 1)
                wait(act, pv_ok, UO * (i - 1))
                act.activation(va[:, par, t, :, 0:HD],
                               QKV_PS[s][:, 2 * GC:3 * GC].rearrange("p (h d) -> p h d", d=HD),
                               ACT.Copy).then_inc(vh_ok, 1)

            def t_high(i, t):
                n = 4 * i + t
                s = t % 2
                wait(act, qp_ok, n + 1)
                wait(act, tk_full, n - 1)
                v = qp[:, s, :].rearrange("p (a h d) -> p h a d", a=2, h=HG)
                act.activation(tt[:, s, :, 0:4:3, :], v, ACT.Copy)
                act.activation(tt[:, s, :, 1:6:4, :], v, ACT.Copy).then_inc(th_ok, 1)

            def t_evac(i, par, t):
                n = 4 * i + t
                if t == 0:
                    wait(act, st_full, UO * (i - 1))
                for full, ev, bank, dst in ((tq_full, tq_ev, X_PS[0], qst), (tk_full, tk_ev, X_PS[1], kst)):
                    wait(act, full, n + 1)
                    act.activation(dst[0:KS, par, :, t * P:(t + 1) * P],
                                   bank[0:KS, :].rearrange("p (h n) -> p h n", h=HG), ACT.Copy).then_inc(ev, 1)

            def exps(i, h, e):
                n = UO * i + NOP * h + e
                s = (NOP * h + e) % NP_
                w = sum(o[2] for o in ST_OPS[e])
                bank = ST_PS[(NOP * h + e) % 2]
                wait(act, st_full, n + 1)
                wait(act, pv_ok, n - NP_ + 1)
                act.activation(pf[:, s, 0:w], bank[:, 0:w], ACT.Exp, scale=SCALE)
                act.activation(ph[:, s, 0:w], bank[:, 0:w], ACT.Exp, scale=SCALE).then_inc(p_ok, 1)

            def o_evac(i, h):
                wait(act, pv_ok, UO * i + NOP * (h + 1))
                if h == 0:
                    wait(act, og_in, 16 * 2 * HG * i)
                    wait(act, d_in, 16 * i)
                act.activation(oraw[:, h, :], PV_PS[0:VW, :], ACT.Copy).then_inc(o_ev, 1)

            def o_high(b, c):
                i = 4 * b + c
                wait(act, on_ok, i + 1)
                if c % 4 == 0:
                    wait(act, wo_full, 4 * b + c - c % 4 - 0 if c < 4 else 4 * (b + 1))
                act.activation(on_h[:, c % 4, :], on[:], ACT.Copy).then_inc(onh_ok, 1)

            def m_evac(i, par):
                wait(act, mt_full, i + 1)
                wait(act, m_in, 16 * i)
                act.activation(mrow[:], X_PS[0][0:HG * TB, 0:P], ACT.Copy, scale=-1.0).then_inc(mt_ok, 1)
                wait(act, mt_ok, i + 1)
                act.dma_start(qst[KS:KS + 1, par, :, :].bitcast(F32).rearrange(
                    "o h (t n) -> o (h t) n", t=TB), mrow[:].bitcast(F32)).then_inc(m_in, 16)

            def s_evac(b, t):
                n = 4 * b + t
                wait(act, wo_full, n + 1)
                act.activation(s_sb[:, t, :], W_PS[:], ACT.Copy).then_inc(s_ev, 1)
                wait(act, s_ev, n + 1)
                dst = s_dram[b, t * P:(t + 1) * P, :] if isinstance(b, int) else \
                    s_dram[bass.ds(b, 1), t * P:(t + 1) * P, :].rearrange("o p d -> (o p) d")
                act.dma_start(dst, s_sb[:, t, :]).then_inc(s_out[t % 2], 16)

            def slot(b, c):
                i, par, i1, par1, b1, g1 = parts(b, c)
                attend = not (isinstance(i, int) and i < 0)
                prep = not last(b, c)
                for k in range(TB):
                    if g1 == 0 and prep:
                        xt_high(b1, k)
                    if prep:
                        square(i1, par1, k)
                    if attend:
                        exps(i, k, 0)
                    if prep and k >= 1:
                        if k >= 2:
                            t_evac(i1, par1, k - 2)
                        t_high(i1, k - 1)
                    if attend:
                        exps(i, k, 1)
                        if k >= 1:
                            o_evac(i, k - 1)
                        exps(i, k, 2)
                    if k == 3 and not (isinstance(i, int) and i < 1):
                        o_high(b, c - 1)
                    if not attend and k < G - 1:
                        split_w(k + 1)
                if prep:
                    t_evac(i1, par1, TB - 2)
                    t_high(i1, TB - 1)
                if attend:
                    o_evac(i, HG - 1)
                if prep:
                    t_evac(i1, par1, TB - 1)
                if not attend:
                    split_w(G)
                    act.wait_ge(w_lo, G + 1)
                if c == 4:
                    for t in range(TB):
                        s_evac(b, t)
                if prep:
                    m_evac(i1, par1)

            split_w(0)
            run_slots(act, slot)
            o_high(B - 1, 3)
            for t in range(TB):
                s_evac(B - 1, t)
            act.sem_inc(a_act, 1)

            act.wait_ge(c2_in, 48)

            def gate(b, m):
                n = MT * b + m
                wait(act, gu_full, n + 1)
                wait_slot(act, hf_ok, n, m)
                act.activation(gs[:, GP(m), :], GU_PS[2 * GP(m)][:], ACT.Silu,
                               scale=sgu[:, 0, m:m + 1]).then_inc(gs_ok, 1)

            def high(b, m):
                n = MT * b + m
                wait(act, hf_ok, n + 1)
                if m == 0:
                    wait(act, dn_full, 4 * b)
                act.activation(ht_h[:, m, :], hf[:, GP(m), :], ACT.Copy).then_inc(hh_ok, 1)

            def outer(b, t):
                n = 4 * b + t
                wait(act, y_ok, n + 1)
                wait_slot(act, sgx_ok, n, t)
                act.activation(gt[:, t % 2, :], yt[:, t % 2, :], ACT.Silu).then_inc(g_ok, 1)

            odd = [0]

            def GP(m):
                return (m + odd[0]) % 2

            with act.Fori(0, B // 2) as bb:
                for e in range(2):
                    odd[0] = e * MT % 2
                    b = 2 * bb + e
                    for m in range(MT):
                        gate(b, m)
                        if m:
                            high(b, m - 1)
                    high(b, MT - 1)
                    for t in range(TB):
                        outer(b, t)

        @block.vector
        def _(dve):
            dve.wait_ge(c_in, 16 * 8)
            dve.tensor_copy(idr[:], idf[:]).then_inc(idr_ok, 1)

            def split_w(g):
                dve.wait_ge(w_hi, g + 1)
                if g < G:
                    cols = slice(g * 3 * GC, (g + 1) * 3 * GC)
                    dve.tensor_tensor(wq_l[:, :, cols], stage[:, :, cols], wq_h[:, :, cols].bitcast(F32),
                                      ALU.subtract).then_inc(w_lo, 1)
                else:
                    dve.tensor_tensor(wo_l[:], stage[:, :, G * 3 * GC:], wo_h[:].bitcast(F32),
                                      ALU.subtract).then_inc(w_lo, 1)

            def ln_stats(b, t):
                n = 4 * b + t
                s = t % 2
                wait(dve, x_in[t], 16 * (b + 1))
                dve.bn_stats(st6[:, s, 0:6], xr[:, t, :]).then_inc(ln_s, 1)
                wait(dve, ln_s, n + 1)
                dve.tensor_copy(st6[:, s, 6:7], st6[:, s, 0:1])
                dve.bn_aggr(mv[:, s, 0:2], st6[:, s, 0:6]).then_inc(ln_a, 1)
                wait(dve, ln_a, n + 1)
                dve.tensor_scalar(ve[:, s, 0:1], mv[:, s, 1:2], LN_EPS, None, ALU.add).then_inc(ln_v, 1)

            def ln_apply(b, t):
                n = 4 * b + t
                s = t % 2
                wait(dve, ln_r, n + 1)
                dve.tensor_scalar(xr[:, t, :], xr[:, t, :], mv[:, s, 0:1], rstd[:, s, 0:1],
                                  ALU.subtract, ALU.mult).then_inc(xn_ok, 1)

            def xt_low(b, t):
                n = 4 * b + t
                wait(dve, xt_hi, n + 1)
                cols = slice(t * P, (t + 1) * P)
                dve.tensor_tensor(xnt_l[:, :, cols], W_PS[:].rearrange("p (k n) -> p k n", k=KT),
                                  xnt_h[:, :, cols].bitcast(F32), ALU.subtract).then_inc(xt_lo, 1)

            def squares(i, t):
                n = 4 * i + t
                s = t % 2
                wait(dve, sq_ok, n + 1)
                wait(dve, rr_ok, n - 1)
                dve.tensor_reduce(ss[:, s, :], sq[:, s], AX.X, ALU.add).then_inc(ss_ok, 1)

            def unit_rms(i, par, t):
                n = 4 * i + t
                s = t % 2
                wait(dve, rr_ok, n + 1)
                wait(dve, rope_ok, n - 1)
                wait(dve, vh_ok, n + 1)
                dve.tensor_tensor(qn[:, s].rearrange("p a h d -> p (a h) d"),
                                  QKV_PS[s][:, 0:2 * GC].rearrange("p (h d) -> p h d", d=HD),
                                  rr[:, s, :].rearrange("p (h o) -> p h o", o=1).to_broadcast([P, 2 * HG, HD]),
                                  ALU.mult).then_inc(qn_ok, 1)
                dve.tensor_tensor(va[:, par, t, :, HD:2 * HD],
                                  QKV_PS[s][:, 2 * GC:3 * GC].rearrange("p (h d) -> p h d", d=HD),
                                  va[:, par, t, :, 0:HD].bitcast(F32), ALU.subtract).then_inc(vl_ok, 1)

            def rope_sum(i, t):
                n = 4 * i + t
                s = t % 2
                wait(dve, rope_ok, n + 1)
                wait(dve, tl_ok, n - 1)
                wait(dve, th_ok, n - 1)
                dve.tensor_tensor(qp[:, s, :], ra[:, s].rearrange("p a h d -> p (a h d)"),
                                  rb[:, s].rearrange("p a h d -> p (a h d)"), ALU.add).then_inc(qp_ok, 1)

            def t_low(i, t):
                n = 4 * i + t
                s = t % 2
                wait(dve, th_ok, n + 1)
                dve.tensor_tensor(tt[:, s, :, 2:5:2, :], qp[:, s, :].rearrange("p (a h d) -> p h a d", a=2, h=HG),
                                  tt[:, s, :, 0:4:3, :].bitcast(F32), ALU.subtract).then_inc(tl_ok, 1)

            def p_low(i, h, e):
                n = UO * i + NOP * h + e
                s = (NOP * h + e) % NP_
                w = sum(o[2] for o in ST_OPS[e])
                wait(dve, p_ok, n + 1)
                dve.tensor_tensor(pl[:, s, 0:w], pf[:, s, 0:w], ph[:, s, 0:w].bitcast(F32),
                                  ALU.subtract).then_inc(pl_ok, 1)

            def maxima(i):
                wait(dve, mt_full, i)
                for h in range(HG):
                    for e, ops in enumerate(SM_OPS):
                        n = NOP * h + e
                        wait(dve, sm_full, UO * i + n + 1)
                        for qb, c0, w in ops:
                            op = dve.tensor_reduce(mx[:, TB * h + qb:TB * h + qb + 1],
                                                   X_PS[n % 2][:, c0:c0 + w], AX.X, ALU.max)
                        op.then_inc(sm_ok, 1)

            def recip(i):
                wait(dve, d_in, 16 * (i + 1))
                wait(dve, rd_out, 16 * i)
                dve.reciprocal(rd16[:], den16[:]).then_inc(rd_ok, 1)

            def o_low(b, c):
                i = 4 * b + c
                wait(dve, onh_ok, i + 1)
                dve.tensor_tensor(on_l[:, c % 4, :], on[:], on_h[:, c % 4, :].bitcast(F32),
                                  ALU.subtract).then_inc(onl_ok, 1)

            def slot(b, c):
                i, par, i1, par1, b1, g1 = parts(b, c)
                attend = not (isinstance(i, int) and i < 0)
                former = not (isinstance(i, int) and i < 1)
                prep = not last(b, c)
                for k in range(TB):
                    if g1 == 0 and prep:
                        xt_low(b1, k)
                    if not attend and k < 2:
                        ln_stats(0, k + 2)
                    if prep:
                        squares(i1, k)
                        if k >= 1:
                            rope_sum(i1, k - 1)
                    if not attend and k < 2:
                        ln_apply(0, k + 2)
                    if attend:
                        p_low(i, k, 0)
                    if prep:
                        unit_rms(i1, par1, k)
                        if k >= 1:
                            t_low(i1, k - 1)
                    if attend:
                        p_low(i, k, 1)
                    if ln_slot(b, c):
                        if k >= 1:
                            ln_apply(b + 1, k - 1)
                        ln_stats(b + 1, k)
                    if k == 1 and former:
                        recip(i - 1)
                    if attend:
                        p_low(i, k, 2)
                    if not attend and k < G - 1:
                        split_w(k + 1)
                if ln_slot(b, c):
                    ln_apply(b + 1, TB - 1)
                if prep:
                    rope_sum(i1, TB - 1)
                    t_low(i1, TB - 1)
                if not attend:
                    split_w(G)
                if former:
                    o_low(b, c - 1)
                if prep:
                    maxima(i1)

            for t in range(2):
                ln_stats(0, t)
            for t in range(2):
                ln_apply(0, t)
            split_w(0)
            run_slots(dve, slot)
            recip(4 * B - 1)
            o_low(B - 1, 3)
            dve.sem_inc(a_dve, 1)

            dve.wait_ge(a_act, 1)
            dve.wait_ge(a_pool, 1)
            dve.wait_ge(wo_full, 4 * B)
            dve.wait_ge(xs_out, 32 * B)
            for m in range(MT):
                dve.wait_ge(ws_in[m % 2], 16 * (m // 2 + 1))
                dve.tensor_scalar(wgu[:, m], wst[:, m % 2, :].rearrange("p (k n) -> p k n", k=KT), -ZERO, None,
                                  ALU.add).then_inc(wc_ok, 1)

            def down_weights():
                for q in range(MT):
                    n = MT + q
                    dve.wait_ge(ws_in[n % 2], 16 * (n // 2 + 1))
                    dve.tensor_scalar(wd[:, q, :], wst[:, n % 2, 0:H], -ZERO, None, ALU.add).then_inc(wc_ok, 1)

            def hidden(b, m, s):
                n = MT * b + m
                wait(dve, gs_ok, n + 1)
                wait_slot(dve, hh_ok, n, m)
                wait_slot(dve, hl_ok, n, m)
                dve.scalar_tensor_tensor(hf[:, s, :], GU_PS[2 * s + 1][:], sgu[:, 1, m:m + 1], gs[:, s, :],
                                         ALU.mult, ALU.mult).then_inc(hf_ok, 1)

            def low(b, m, s):
                n = MT * b + m
                wait(dve, hh_ok, n + 1)
                dve.tensor_tensor(ht_l[:, m, :], hf[:, s, :], ht_h[:, m, :].bitcast(F32),
                                  ALU.subtract).then_inc(hl_ok, 1)

            def scaled(b, t):
                n = 4 * b + t
                wait(dve, dn_full, n + 1)
                wait_slot(dve, g_ok, n, t)
                dve.tensor_tensor(yt[:, t % 2, :], DN_PS[t][:], sdb[:], ALU.mult).then_inc(y_ok, 1)

            def finish(b, t):
                n = 4 * b + t
                s = t % 2
                wait(dve, g_ok, n + 1)
                wait(dve, xs_in[s], 32 * (2 * b + t // 2 + 1))
                wait(dve, r_out[s], 16 * (2 * b + t // 2))
                dve.tensor_tensor(res[:, s, :], gt[:, s, :], xs[:, s, 1, :], ALU.mult).then_inc(sgx_ok, 1)
                wait(dve, sgx_ok, n + 1)
                dve.tensor_tensor(res[:, s, :], res[:, s, :], xs[:, s, 0, :], ALU.add).then_inc(res_ok, 1)

            dve.wait_ge(c2_in, 48)
            down_weights()
            with dve.Fori(0, B // 2) as bb:
                for e in range(2):
                    b = 2 * bb + e
                    for m in range(MT):
                        s = (m + e * MT) % 2
                        hidden(b, m, s)
                        if m:
                            low(b, m - 1, 1 - s)
                    low(b, MT - 1, s)
                    for t in range(TB):
                        scaled(b, t)
                        if t:
                            finish(b, t - 1)
                    finish(b, TB - 1)

        @block.tensor
        def _(pe):
            pe.wait_ge(c_in, 16 * 8)
            pe.wait_ge(idr_ok, 1)
            pe.wait_ge(ones_ok, 4)

            def xn_turn(b, t):
                n = 4 * b + t
                wait(pe, xn_ok, n + 1)
                wait(pe, xt_lo, n)
                wait(pe, s_ev, 4 * (b - 1))
                for k in range(KT):
                    op = pe.transpose(W_PS[:, k * P:(k + 1) * P], xr[:, t, k * P:(k + 1) * P], idf[:])
                op.then_inc(xt_full, 1)

            def project(i, b, g, t):
                n = 4 * i + t
                if g == 0:
                    wait(pe, xt_hi, 4 * b + t + 1)
                    wait(pe, xt_lo, 4 * b + t + 1)
                if isinstance(i, int):
                    pe.wait_ge(w_lo, g + 1)
                wait(pe, sq_ok, n - 1)
                wait(pe, vh_ok, n - 1)
                wait(pe, vl_ok, n - 1)
                cols = slice(g * 3 * GC, (g + 1) * 3 * GC)
                todo = [(x_, w_, k) for x_, w_ in ((xnt_h, wq_h), (xnt_l, wq_h), (xnt_h, wq_l)) for k in range(KT)]
                for j, (x_, w_, k) in enumerate(todo):
                    op = pe.matmul(QKV_PS[t % 2][:, 0:3 * GC], x_[:, k, t * P:(t + 1) * P], w_[:, k, cols],
                                   start=(j == 0), stop=(j == len(todo) - 1))
                op.then_inc(qkv_full, 1)

            def turn(i, t):
                n = 4 * i + t
                s = t % 2
                wait(pe, tl_ok, n + 1)
                if t == 0:
                    wait(pe, mt_ok, i)
                    wait(pe, sm_ok, UO * i)
                for a, full, ev in ((0, tq_full, tq_ev), (1, tk_full, tk_ev)):
                    if t:
                        wait(pe, ev, n)
                    for h in range(HG):
                        op = pe.transpose(X_PS[a][0:KS, h * P:(h + 1) * P].bitcast(F32R),
                                          tt[:, s, h, 3 * a:3 * a + 3, :].rearrange("p c d -> p (c d)"), idr[:])
                    op.then_inc(full, 1)

            def scores_t(i, par, h, e):
                n = UO * i + NOP * h + e
                wait(pe, p_ok, n - 1)
                bank = ST_PS[(NOP * h + e) % 2]
                for j, c0, w in ST_OPS[e]:
                    pe.matmul(bank[:, c0:c0 + w], kst[0:KS + 1, par, h, j * P:(j + 1) * P],
                              qst[0:KS + 1, par, h, j * P:N], start=True, stop=False)
                    op = pe.matmul(bank[:, c0:c0 + P], idb[:], msk_t[:], start=False, stop=True)
                op.then_inc(st_full, 1)

            def p_v(i, par, h, e):
                n = UO * i + NOP * h + e
                s = (NOP * h + e) % NP_
                wait(pe, pl_ok, n + 1)
                if e == 0:
                    wait(pe, o_ev, 4 * i + h)
                for j, c0, w in ST_OPS[e]:
                    for part in (ph, pl):
                        op = pe.matmul(PV_PS[0:VW, j * P:N], va[:, par, j, h, :], part[:, s, c0:c0 + w],
                                       start=(j == 0 and part is ph), stop=(j == 2 and part is pl))
                op.then_inc(pv_ok, 1)

            def maxima(i, par):
                for h in range(HG):
                    for e, ops in enumerate(SM_OPS):
                        n = NOP * h + e
                        if n == 0:
                            wait(pe, tq_ev, 4 * i + 4)
                            wait(pe, tk_ev, 4 * i + 4)
                        else:
                            wait(pe, sm_ok, UO * i + n - 1)
                        bank = X_PS[n % 2]
                        for qb, c0, w in ops:
                            pe.matmul(bank[:, c0:c0 + w], qst[0:KS, par, h, qb * P:(qb + 1) * P],
                                      kst[0:KS, par, h, 0:w], start=True, stop=False)
                            op = pe.matmul(bank[:, c0 + w - P:c0 + w], idb[:], msk_s[:], start=False, stop=True)
                        op.then_inc(sm_full, 1)
                wait(pe, sm_ok, UO * i + UO)
                pe.transpose(X_PS[0][0:HG * TB, 0:P], mx[:], idf[:]).then_inc(mt_full, 1)

            def out_proj(b, t, ahead):
                n = 4 * b + t
                if t == 0:
                    wait(pe, onl_ok, 4 * b + 4)
                    wait(pe, xt_lo, 4 * (b + 1 + ahead))
                    pe.wait_ge(w_lo, G + 1)
                wait(pe, s_ev, n)
                todo = [(o_, w_, g) for o_, w_ in ((on_h, wo_h), (on_l, wo_h), (on_h, wo_l)) for g in range(G)]
                for j, (o_, w_, g) in enumerate(todo):
                    op = pe.matmul(W_PS[:], o_[:, g, t * P:(t + 1) * P], w_[:, g, :],
                                   start=(j == 0), stop=(j == len(todo) - 1))
                op.then_inc(wo_full, 1)

            def slot(b, c):
                i, par, i1, par1, b1, g1 = parts(b, c)
                attend = not (isinstance(i, int) and i < 0)
                prep = not last(b, c)
                if attend:
                    wait(pe, m_in, 16 * (i + 1))
                    wait(pe, vl_ok, 4 * (i + 1))
                for k in range(TB):
                    if prep:
                        if g1 == 0:
                            xn_turn(b1, k)
                        project(i1, b1, g1, k)
                    if attend:
                        for e in range(NOP):
                            scores_t(i, par, k, e)
                            q = NOP * k + e - 2
                            if q >= 0:
                                p_v(i, par, q // NOP, q % NOP)
                    if prep and k >= 1:
                        turn(i1, k - 1)
                if attend:
                    for q in (UO - 2, UO - 1):
                        p_v(i, par, q // NOP, q % NOP)
                if prep:
                    turn(i1, TB - 1)
                if c == 4:
                    for t in range(TB):
                        out_proj(b, t, 1)
                if prep:
                    maxima(i1, par1)

            run_slots(pe, slot)
            for t in range(TB):
                out_proj(B - 1, t, 0)
            pe.wait_ge(s_ev, 4 * B)

            def gate_up(b, par, m, s):
                n = MT * b + m
                wait(pe, wc_ok, m + 1)
                wait_slot(pe, hf_ok, n, m)
                for a in range(2):
                    todo = [(x_, k) for x_ in (xb_h, xb_l) for k in range(KT)]
                    for j, (x_, k) in enumerate(todo):
                        op = pe.matmul(GU_PS[2 * s + a][:], wgu[:, m, k, a * P:(a + 1) * P], x_[:, par, k, :],
                                       start=(j == 0), stop=(j == len(todo) - 1))
                op.then_inc(gu_full, 1)

            def down(b, t):
                n = 4 * b + t
                wait_slot(pe, y_ok, n, t, TB)
                if t == 0:
                    pe.wait_ge(wc_ok, 2 * MT)
                for m in range(MT):
                    if t == 0:
                        wait(pe, hl_ok, MT * b + m + 1)
                    for h_ in (ht_h, ht_l):
                        op = pe.matmul(DN_PS[t][:], h_[:, m, t * P:(t + 1) * P], wd[:, m, :],
                                       start=(m == 0 and h_ is ht_h), stop=(m == MT - 1 and h_ is ht_l))
                op.then_inc(dn_full, 1)

            with pe.Fori(0, B // 2) as bb:
                for e in range(2):
                    b = 2 * bb + e
                    wait(pe, xb_in[e], 32 * (bb + 1))
                    for m in range(MT):
                        gate_up(b, e, m, (m + e * MT) % 2)
                    for t in range(TB):
                        down(b, t)


def kernel(L0_attn_x, L0_attn_w_qkv, L0_attn_w_out, L0_attn_q_gamma, L0_attn_k_gamma,
           L0_ffn_wq_gate, L0_ffn_s_gate, L0_ffn_wq_up, L0_ffn_s_up, L0_ffn_wq_down, L0_ffn_s_down):
    import ml_dtypes
    import concourse.bacc as bacc
    from concourse.bass_utils import run_bass_kernel_spmd

    def ar(a):
        return np.asarray(a)

    inv = (1.0 / np.float32(THETA) ** (np.arange(0, HD, 2, dtype=np.float32) / np.float32(HD))).astype(np.float32)
    ang = np.arange(N, dtype=np.float32)[:, None] * inv[None, :]
    ang = np.concatenate([ang, ang], -1)
    sign = np.where(np.arange(HD) < HD // 2, -1.0, 1.0)
    root = np.sqrt(float(HD))
    cos_tab = (np.cos(ang.astype(np.float64)) * root).astype(np.float32)
    sin_tab = (np.sin(ang.astype(np.float64)) * sign * root).astype(np.float32)
    tri = np.arange(P)
    arrays = {
        "x": np.ascontiguousarray(ar(L0_attn_x)),
        "w_qkv": np.ascontiguousarray(ar(L0_attn_w_qkv).reshape(KT, P, 3, G, GC).transpose(1, 0, 3, 2, 4)
                                      .reshape(P, KT, G * 3 * GC)),
        "w_out": np.ascontiguousarray(ar(L0_attn_w_out).reshape(KT, P, H).transpose(1, 0, 2)),
        "q_gamma": ar(L0_attn_q_gamma).reshape(1, HD),
        "k_gamma": ar(L0_attn_k_gamma).reshape(1, HD),
        "w_gu": np.ascontiguousarray(np.stack([ar(w).reshape(MT, P, KT, P).transpose(0, 3, 2, 1)
                                               for w in (L0_ffn_wq_gate, L0_ffn_wq_up)], 3).reshape(MT, P, KT, 2 * P)),
        "s_gate": np.ascontiguousarray(ar(L0_ffn_s_gate).reshape(MT, P).T),
        "s_up": np.ascontiguousarray(ar(L0_ffn_s_up).reshape(MT, P).T),
        "w_down": np.ascontiguousarray(ar(L0_ffn_wq_down).T.reshape(MT, P, H)),
        "s_down": ar(L0_ffn_s_down).reshape(1, H),
        "cos_tab": np.ascontiguousarray(cos_tab.reshape(TB, P, HD).transpose(1, 0, 2)),
        "sin_tab": np.ascontiguousarray(sin_tab.reshape(TB, P, HD).transpose(1, 0, 2)),
        "ident": np.eye(P, dtype=np.float32),
        "ident_b": np.eye(P, dtype=np.float32).astype(ml_dtypes.bfloat16),
        "mask_s": np.where(tri[None, :] > tri[:, None], NEG, 0.0).astype(ml_dtypes.bfloat16),
        "mask_t": np.where(tri[:, None] > tri[None, :], NEG, 0.0).astype(ml_dtypes.bfloat16),
    }
    nc = bacc.Bacc("TRN2", target_bir_lowering=False, num_devices=1)
    d = {k: nc.dram_tensor(k, a.shape, mybir.dt.from_np(a.dtype), kind="ExternalInput").ap()
         for k, a in arrays.items()}
    s_dram = nc.dram_tensor("s_dram", (B, N, H), F32, kind="Internal").ap()
    rd_dram = nc.dram_tensor("rd_dram", (1, HG * N), F32, kind="Internal").ap()
    xnt_dram = nc.dram_tensor("xnt_dram", (2, B, P, KT, N), F32, kind="Internal").ap()
    out = nc.dram_tensor("out", (B, N, H), F32, kind="ExternalOutput").ap()
    build(nc, d["x"], d["w_qkv"], d["w_out"], d["q_gamma"], d["k_gamma"], d["w_gu"], d["s_gate"], None,
          d["s_up"], d["w_down"], d["s_down"], d["cos_tab"], d["sin_tab"], d["ident"], d["ident_b"],
          d["mask_s"], d["mask_t"], s_dram, rd_dram, xnt_dram, out)
    r = run_bass_kernel_spmd(nc, [arrays], core_ids=[0])
    return r.results[0]["out"]
```

```python
from contextlib import ExitStack

import numpy as np

import concourse.bass as bass
from concourse import mybir

ALU = mybir.AluOpType
ACT = mybir.ActivationFunctionType
AX = mybir.AxisListType
F32 = mybir.dt.float32
F32R = mybir.dt.float32r
BF16 = mybir.dt.bfloat16
I32 = mybir.dt.int32

B, N, H = 4, 512, 512
NH = 16
HD = H // NH
P = 128
TB = N // P
KT = H // P
G = 4
HG = NH // G
GC = HG * HD
HID = 1408
MT = HID // P
LN_EPS, RMS_EPS, THETA, NEG, ZERO = 1e-5, 1e-6, 10000.0, -1e30, 128.0
SCALE = 1.0 / float(np.sqrt(HD))
VW = 2 * HD + 1
KS = 3 * HD
VR = 4
ST_OPS = [[(0, 0, 512)], [(1, 0, 384), (3, 384, 128)], [(2, 0, 256)]]
SM_OPS = [[(0, 1, 2, 3)], [(0, 1), (2, 3)], [(0,), (1,), (2,), (3,)], [(0,), (1,), (2,), (3,)]]
SM_BASE = [sum(len(o) for o in SM_OPS[:t]) for t in range(TB)]
SM_UNIT = sum(len(o) for o in SM_OPS)
NOP = len(ST_OPS)
UO = HG * NOP


def wait(eng, sem, value):
    if isinstance(value, int) and value <= 0:
        return
    eng.wait_ge(sem, value)


def wait_slot(eng, sem, n, pos, ring=2):
    value = n - pos if pos < ring - 1 else n - ring + 1
    if isinstance(value, int) and value <= 0:
        return
    eng.wait_ge(sem, value)


def build(nc, x, w_qkv, w_out, q_gamma, k_gamma, w_gate, s_gate, w_up, s_up, w_down, s_down,
          cos_tab, sin_tab, ident, ident_b, mask_s, mask_t, s_dram, rd_dram, xnt_dram, out):
    top = ExitStack()
    with top:
        def sem(name):
            return top.enter_context(nc.semaphore(name))

        def tiles(stack):
            def sb(name, shape, dt=F32):
                return stack.enter_context(nc.sbuf_tensor(name, shape, dt))
            return sb

        psum = [top.enter_context(nc.psum_tensor(f"bank{n}", [P, 512], F32)) for n in range(8)]
        QKV_PS, X_PS, W_PS, ST_PS, PV_PS = psum[0:2], psum[2:4], psum[4], psum[5:7], psum[7]
        GU_PS, DN_PS = psum[0:4], psum[4:8]

        pa = ExitStack()
        sb = tiles(pa)
        wq_h = sb("wq_h", [P, KT, G * 3 * GC], F32R)
        wq_l = sb("wq_l", [P, KT, G * 3 * GC], F32R)
        wo_h = sb("wo_h", [P, KT, H], F32R)
        wo_l = sb("wo_l", [P, KT, H], F32R)
        xnt_h = sb("xnt_h", [P, KT, N], F32R)
        xnt_l = sb("xnt_l", [P, KT, N], F32R)
        idf = sb("idf", [P, P])
        idr = sb("idr", [P, P], F32R)
        idb = sb("idb", [P, P], BF16)
        msk_s = sb("msk_s", [P, P], BF16)
        msk_t = sb("msk_t", [P, P], BF16)
        gam = sb("gam", [P, 2, HD])
        cg = sb("cg", [P, TB, 2, HD])
        sg = sb("sg", [P, TB, 2, HD])
        half = sb("half", [P, 8])
        xr = sb("xr", [P, TB, H])
        st6 = sb("st6", [P, 2, 8])
        mv = sb("mv", [P, 2, 8])
        ve = sb("ve", [P, 2, 8])
        rstd = sb("rstd", [P, 2, 8])
        sq = sb("sq", [P, 2, 2 * HG, HD + 1])
        ss = sb("ss", [P, 2, 8])
        rr = sb("rr", [P, 2, 8])
        qn = sb("qn", [P, 2, 2, HG, HD])
        ra = sb("ra", [P, 2, 2, HG, HD])
        rb = sb("rb", [P, 2, 2, HG, HD])
        ctab, stab = rb[:, 0, 0], rb[:, 0, 1]
        qp = sb("qp", [P, 2, 2 * GC])
        tt = sb("tt", [P, 2, HG, 6, HD], F32R)
        qst = sb("qst", [P, 2, HG, N], F32R)
        kst = sb("kst", [P, 2, HG, N], F32R)
        va = sb("va", [P, VR, TB, HG, VW], F32R)
        mx = sb("mx", [P, HG * TB])
        mrow = sb("mrow", [HG * TB, P], F32R)
        den16 = sb("den16", [P, HG * TB])
        rd16 = sb("rd16", [P, HG * TB])
        with ExitStack() as early:
            stage = tiles(early)("stage", [P, KT, G * 3 * GC + H])
        pf = sb("pf", [P, NOP, 512])
        ph = sb("ph", [P, NOP, 512], F32R)
        pl = sb("pl", [P, NOP, 512], F32R)
        oraw = sb("oraw", [VW, HG, N])
        oh = sb("oh", [P, N])
        ol = sb("ol", [P, N])
        rdb = sb("rdb", [P, N])
        on = sb("on", [P, N])
        on_h = sb("on_h", [P, G, N], F32R)
        on_l = sb("on_l", [P, G, N], F32R)
        s_sb = xr
        pa.close()

        pbs = ExitStack()
        sb = tiles(pbs)
        wgu = sb("wgu", [P, MT, KT, 2 * P], F32R)
        wd = sb("wd", [P, MT, H], F32R)
        xb_h = sb("xb_h", [P, 2, KT, N], F32R)
        xb_l = sb("xb_l", [P, 2, KT, N], F32R)
        ht_h = sb("ht_h", [P, MT, N], F32R)
        ht_l = sb("ht_l", [P, MT, N], F32R)
        wst = sb("wst", [P, 2, KT * 2 * P], I32)
        sgu = sb("sgu", [P, 2, MT])
        sdb = sb("sdb", [P, H])
        gs = sb("gs", [P, 2, N])
        hf = sb("hf", [P, 2, N])
        yt = sb("yt", [P, 2, H])
        gt = sb("gt", [P, 2, H])
        xs = sb("xs", [P, 2, 2, H])
        res = sb("res", [P, 2, H])
        pbs.close()

        c_in = sem("c_in")
        w_in = [sem(f"w_in{g}") for g in range(G + 1)]
        w_hi, w_lo = sem("w_hi"), sem("w_lo")
        idr_ok, ones_ok, tab_c, tab_ok = sem("idr_ok"), sem("ones_ok"), sem("tab_c"), sem("tab_ok")
        x_in = [sem(f"x_in{t}") for t in range(TB)]
        ln_s, ln_a, ln_v, ln_r = sem("ln_s"), sem("ln_a"), sem("ln_v"), sem("ln_r")
        xn_ok, xt_full, xt_hi, xt_lo = sem("xn_ok"), sem("xt_full"), sem("xt_hi"), sem("xt_lo")
        xs_out = sem("xs_out")
        qkv_full, sq_ok, vh_ok, ss_ok, rr_ok = (sem(n) for n in ("qkv_full", "sq_ok", "vh_ok", "ss_ok", "rr_ok"))
        qn_ok, vl_ok, rope_ok, qp_ok = (sem(n) for n in ("qn_ok", "vl_ok", "rope_ok", "qp_ok"))
        th_ok, tl_ok, tq_full, tk_full = (sem(n) for n in ("th_ok", "tl_ok", "tq_full", "tk_full"))
        tq_ev, tk_ev = sem("tq_ev"), sem("tk_ev")
        sm_full, sm_ok, mt_full, mt_ok, m_in = (sem(n) for n in ("sm_full", "sm_ok", "mt_full", "mt_ok", "m_in"))
        st_full, p_ok, pl_ok, pv_ok, o_ev = (sem(n) for n in ("st_full", "p_ok", "pl_ok", "pv_ok", "o_ev"))
        og_in, d_in, rd_ok, rd_out, rb_in = (sem(n) for n in ("og_in", "d_in", "rd_ok", "rd_out", "rb_in"))
        os_ok, on_ok, onh_ok, onl_ok = (sem(n) for n in ("os_ok", "on_ok", "onh_ok", "onl_ok"))
        wo_full, s_ev = sem("wo_full"), sem("s_ev")
        s_out = [sem("s_out0"), sem("s_out1")]
        a_act, a_dve, a_pool = sem("a_act"), sem("a_dve"), sem("a_pool")
        ws_in = [sem("ws_in0"), sem("ws_in1")]
        wc_ok, wd_ok, c2_in = sem("wc_ok"), sem("wd_ok"), sem("c2_in")
        xb_in = [sem("xb_in0"), sem("xb_in1")]
        gu_full, gs_ok, hf_ok, hh_ok, hl_ok = (sem(n) for n in ("gu_full", "gs_ok", "hf_ok", "hh_ok", "hl_ok"))
        dn_full, y_ok, g_ok, sgx_ok, res_ok = (sem(n) for n in ("dn_full", "y_ok", "g_ok", "sgx_ok", "res_ok"))
        xs_in = [sem("xs_in0"), sem("xs_in1")]
        r_out = [sem("r_out0"), sem("r_out1")]

        block = top.enter_context(nc.Block())

        def run_beats(eng, beat):
            for c in range(-8, 8):
                beat(0, c)
            with eng.Fori(0, B - 1) as r:
                for c in range(8, 24):
                    beat(r, c)
            for c in range(8, 23):
                beat(B - 1, c)

        def there(index, count):
            return not isinstance(index, int) or 0 <= index < count

        NB = B * G * TB

        def at(c, first):
            d, t = divmod(c - first, 16)
            return (d, t) if t < TB else (0, None)

        def sm_count(r, c):
            return SM_UNIT * 4 * r + SM_UNIT * (c // 4) + SM_BASE[c % 4]

        @block.sync
        def _(sp):
            def load_x(b, t):
                sp.dma_start(xr[:, t, :], x[b, t * P:(t + 1) * P, :]
                             if isinstance(b, int) else
                             x[bass.ds(b, 1), t * P:(t + 1) * P, :].rearrange("o p d -> (o p) d")
                             ).then_inc(x_in[t], 16)

            load_x(0, 0)
            load_x(0, 1)
            sp.dma_start(idf[:], ident).then_inc(c_in, 16)
            sp.dma_start(stage[:, :, 0:3 * GC], w_qkv[:, :, 0:3 * GC]).then_inc(w_in[0], 16)
            load_x(0, 2)
            load_x(0, 3)
            for g in range(1, G):
                sp.dma_start(stage[:, :, g * 3 * GC:(g + 1) * 3 * GC],
                             w_qkv[:, :, g * 3 * GC:(g + 1) * 3 * GC]).then_inc(w_in[g], 16)
            sp.dma_start(stage[:, :, G * 3 * GC:], w_out).then_inc(w_in[G], 16)

            def gather(i, h):
                wait(sp, o_ev, 4 * i + h + 1)
                wait(sp, os_ok, i)
                sp.dma_start(oh[HD * h:HD * h + HD, :], oraw[0:HD, h, :]).then_inc(og_in, 16)
                sp.dma_start(ol[HD * h:HD * h + HD, :], oraw[HD:2 * HD, h, :]).then_inc(og_in, 16)

            def den_out(i):
                wait(sp, rd_ok, i)
                sp.dma_start(den16[:], oraw[2 * HD:VW, :, :].rearrange("o h (a n) -> o (h a) n", n=HG * TB)
                             ).then_inc(d_in, 16)

            def den_in(i):
                wait(sp, rd_ok, i + 1)
                sp.dma_start(rd_dram[0:1, :].rearrange("o (p n) -> (o p) n", n=HG * TB),
                             rd16[:]).then_inc(rd_out, 16)
                wait(sp, rd_out, 16 * (i + 1))
                wait(sp, on_ok, i)
                sp.dma_start(rdb[:], rd_dram.rearrange("o (h n) -> (o h) n", h=HG).rearrange(
                    "h (o n) -> h o n", o=1).to_broadcast([HG, HD, N])).then_inc(rb_in, 16)

            def beat(r, c):
                if c == 8 and there(r + 1, B):
                    stored, turned = sp.snap(32 * r), sp.snap(4 * (r + 1))
                    wait(sp, s_out[0], stored)
                    wait(sp, s_out[1], stored)
                    wait(sp, xt_full, turned)
                    for t in range(TB):
                        load_x(r + 1, t)
                if there(16 * r + c - 1, NB):
                    i, h = 4 * r + (c - 1) // 4, (c - 1) % 4
                    gather(i, h)
                    if h == HG - 1:
                        den_out(i)
                        den_in(i)
                d, t = at(c, 9)
                if t == TB - 1 and there(r + 1 + d, B):
                    nb = r + 1 + d
                    wait(sp, xt_hi, 4 * nb + 4)
                    wait(sp, xt_lo, 4 * nb + 4)
                    for n, t_ in ((0, xnt_h), (1, xnt_l)):
                        dst = xnt_dram[n, nb] if isinstance(nb, int) else \
                            xnt_dram[n, bass.ds(nb, 1)].rearrange("o p k n -> (o p) k n")
                        sp.dma_start(dst, t_[:].bitcast(F32)).then_inc(xs_out, 16)

            run_beats(sp, beat)
            sp.wait_ge(a_act, 1)
            sp.wait_ge(a_dve, 1)
            sp.wait_ge(a_pool, 1)
            sp.wait_ge(wo_full, 4 * B)
            sp.wait_ge(s_out[0], 16 * 2 * B)
            sp.wait_ge(s_out[1], 16 * 2 * B)
            sp.wait_ge(xs_out, 32 * B)

            def load_xb(b, par):
                for n, t in ((0, xb_h), (1, xb_l)):
                    src = xnt_dram[n, b] if isinstance(b, int) else \
                        xnt_dram[n, bass.ds(b, 1)].rearrange("o p k n -> (o p) k n")
                    sp.dma_start(t[:, par].bitcast(F32), src).then_inc(xb_in[par], 16)

            load_xb(0, 0)
            for m in range(MT):
                if m >= 2:
                    sp.wait_ge(wc_ok, m - 1)
                sp.dma_start(wst[:, m % 2, :], w_gate[m].rearrange("p k n -> p (k n)")).then_inc(ws_in[m % 2], 16)
                if m == 0:
                    sp.dma_start(sgu[:, 0, :], s_gate).then_inc(c2_in, 16)
                    sp.dma_start(sgu[:, 1, :], s_up).then_inc(c2_in, 16)
                    sp.dma_start(sdb[:], s_down.to_broadcast([P, H])).then_inc(c2_in, 16)
            for q in range(MT):
                n = MT + q
                sp.wait_ge(wc_ok, n - 1)
                sp.dma_start(wst[:, n % 2, 0:H], w_down[q]).then_inc(ws_in[n % 2], 16)

            def load_xs(b, t):
                n = 4 * b + t
                wait_slot(sp, res_ok, n, t)
                rows = slice(t * P, (t + 1) * P)
                for a, src in ((0, x), (1, s_dram)):
                    v = src[b, rows, :] if isinstance(b, int) else \
                        src[bass.ds(b, 1), rows, :].rearrange("o p d -> (o p) d")
                    sp.dma_start(xs[:, t % 2, a, :], v).then_inc(xs_in[t % 2], 16)

            def store(b, t):
                n = 4 * b + t
                wait(sp, res_ok, n + 1)
                v = out[bass.ds(b, 1), t * P:(t + 1) * P, :].rearrange("o p d -> (o p) d")
                sp.dma_start(v, res[:, t % 2, :]).then_inc(r_out[t % 2], 16)

            with sp.Fori(0, B // 2) as bb:
                for e in range(2):
                    b = 2 * bb + e
                    if e == 0:
                        wait(sp, gu_full, MT * (2 * bb))
                        load_xb(b + 1, 1)
                    else:
                        wait(sp, gu_full, MT * (2 * bb + 1))
                        load_xb(2, 0)
                    for t in range(TB):
                        load_xs(b, t)
                        if t >= 1:
                            store(b, t - 1)
                    store(b, TB - 1)
            for n in range(2):
                sp.wait_ge(r_out[n], 16 * 2 * B)
                sp.wait_ge(xb_in[n], 32 * (B // 2 + (n == 0)))

        @block.gpsimd
        def _(pool):
            pool.memset(kst[KS:KS + 1, :, :, :].bitcast(F32), 1.0).then_inc(ones_ok, 1)
            pool.wait_ge(ones_ok, 1)
            pool.memset(half[:], -0.5).then_inc(ones_ok, 1)
            pool.memset(sq[:, :, :, HD:HD + 1], HD * RMS_EPS).then_inc(ones_ok, 1)
            pool.memset(va[:, :, :, :, 2 * HD:VW].bitcast(F32), 1.0).then_inc(ones_ok, 1)
            pool.wait_ge(c_in, 16 * 8)
            for a in range(2):
                for t in range(TB):
                    pool.tensor_tensor(cg[:, t, a, :], ctab[:, t, :], gam[:, a, :], ALU.mult).then_inc(tab_ok, 1)
                    for lo, hi in ((0, HD // 2), (HD // 2, 0)):
                        pool.tensor_tensor(sg[:, t, a, lo:lo + HD // 2], stab[:, t, lo:lo + HD // 2],
                                           gam[:, a, hi:hi + HD // 2], ALU.mult).then_inc(tab_ok, 1)
            pool.wait_ge(tab_ok, 2 * TB * 3)

            def rstd_block(b, t):
                n = 4 * b + t
                wait(pool, ln_v, n + 1)
                pool.tensor_tensor(rstd[:, t % 2, 0:1], ve[:, t % 2, 0:1], half[:, 0:1], ALU.pow).then_inc(ln_r, 1)

            def inv_rms(n, s):
                wait(pool, ss_ok, n + 1)
                pool.tensor_tensor(rr[:, s, :], ss[:, s, :], half[:], ALU.pow).then_inc(rr_ok, 1)

            def rope(n, s, t):
                wait(pool, qn_ok, n + 1)
                wait(pool, qp_ok, n - 1)
                hh = HD // 2
                for a in range(2):
                    pool.tensor_tensor(ra[:, s, a], qn[:, s, a],
                                       cg[:, t, a, :].rearrange("p (o d) -> p o d", o=1).to_broadcast([P, HG, HD]), ALU.mult)
                for a in range(2):
                    for lo, hi in ((0, hh), (hh, 0)):
                        op = pool.tensor_tensor(
                            rb[:, s, a, :, lo:lo + hh], qn[:, s, a, :, hi:hi + hh],
                            sg[:, t, a, lo:lo + hh].rearrange("p (o d) -> p o d", o=1).to_broadcast([P, HG, hh]), ALU.mult)
                op.then_inc(rope_ok, 1)

            def norm(i):
                wait(pool, og_in, 16 * 2 * HG * (i + 1))
                wait(pool, onl_ok, i)
                pool.tensor_tensor(on[:], oh[:], ol[:], ALU.add).then_inc(os_ok, 1)
                wait(pool, os_ok, i + 1)
                wait(pool, rb_in, 16 * (i + 1))
                pool.tensor_tensor(on[:], on[:], rdb[:], ALU.mult).then_inc(on_ok, 1)

            def beat(r, c):
                if there(16 * r + c + 5, NB):
                    rope(16 * r + c + 5, (c + 5) % 2, (c + 5) % 4)
                if (c - 6) % 4 == 0 and there(4 * r + (c - 6) // 4, B * G):
                    norm(4 * r + (c - 6) // 4)
                if there(16 * r + c + 6, NB):
                    inv_rms(16 * r + c + 6, (c + 6) % 2)
                d, t = at(c, 8)
                if t is not None and there(r + 1 + d, B):
                    rstd_block(r + 1 + d, t)

            run_beats(pool, beat)
            pool.sem_inc(a_pool, 1)

        @block.scalar
        def _(act):
            for dst, src in ((idb[:], ident_b), (msk_s[:], mask_s), (msk_t[:], mask_t), (ctab, cos_tab),
                             (stab, sin_tab), (gam[:, 0, :], q_gamma.to_broadcast([P, HD])),
                             (gam[:, 1, :], k_gamma.to_broadcast([P, HD]))):
                act.dma_start(dst, src).then_inc(c_in, 16)

            def split_w(g):
                act.wait_ge(w_in[g], 16)
                if g < G:
                    cols = slice(g * 3 * GC, (g + 1) * 3 * GC)
                    act.activation(wq_h[:, :, cols], stage[:, :, cols], ACT.Copy).then_inc(w_hi, 1)
                else:
                    act.activation(wo_h[:], stage[:, :, G * 3 * GC:], ACT.Copy).then_inc(w_hi, 1)

            def xt_high(b, t):
                n = 4 * b + t
                wait(act, xt_full, n + 1)
                if t == 0:
                    wait(act, xs_out, 32 * b)
                wait(act, qkv_full, 4 * (4 * b - 1) + t + 1)
                act.activation(xnt_h[:, :, t * P:(t + 1) * P], W_PS[:].rearrange("p (k n) -> p k n", k=KT),
                               ACT.Copy).then_inc(xt_hi, 1)

            def square(n, s, v, t):
                wait(act, qkv_full, n + 1)
                wait(act, ss_ok, n - 1)
                act.activation(sq[:, s, :, 0:HD], QKV_PS[s][:, 0:2 * GC].rearrange("p (h d) -> p h d", d=HD),
                               ACT.Square).then_inc(sq_ok, 1)
                wait(act, pv_ok, NOP * (n - t) - UO * (VR - 1))
                act.activation(va[:, v, t, :, 0:HD],
                               QKV_PS[s][:, 2 * GC:3 * GC].rearrange("p (h d) -> p h d", d=HD),
                               ACT.Copy).then_inc(vh_ok, 1)

            def t_high(n, s):
                wait(act, qp_ok, n + 1)
                wait(act, tk_full, n - 1)
                v = qp[:, s, :].rearrange("p (a h d) -> p h a d", a=2, h=HG)
                act.activation(tt[:, s, :, 0:4:3, :], v, ACT.Copy)
                act.activation(tt[:, s, :, 1:6:4, :], v, ACT.Copy).then_inc(th_ok, 1)

            def t_evac(n, par, t):
                if t == 0:
                    wait(act, st_full, NOP * n - UO)
                for full, ev, bank, dst in ((tq_full, tq_ev, X_PS[0], qst), (tk_full, tk_ev, X_PS[1], kst)):
                    wait(act, full, n + 1)
                    act.activation(dst[0:KS, par, :, t * P:(t + 1) * P],
                                   bank[0:KS, :].rearrange("p (h n) -> p h n", h=HG), ACT.Copy).then_inc(ev, 1)

            def exps(j, c, e):
                w = sum(o[2] for o in ST_OPS[e])
                bank = ST_PS[(NOP * c + e) % 2]
                n = NOP * j + e
                wait(act, st_full, n + 1)
                wait(act, pv_ok, n - NOP + 1)
                act.activation(pf[:, e, 0:w], bank[:, 0:w], ACT.Exp, scale=SCALE)
                act.activation(ph[:, e, 0:w], bank[:, 0:w], ACT.Exp, scale=SCALE).then_inc(p_ok, 1)

            def o_evac(j, i, h):
                wait(act, pv_ok, NOP * (j + 1))
                if h == 0:
                    wait(act, og_in, 16 * 2 * HG * i)
                    wait(act, d_in, 16 * i)
                act.activation(oraw[:, h, :], PV_PS[0:VW, :], ACT.Copy).then_inc(o_ev, 1)

            def o_high(i, g):
                wait(act, on_ok, i + 1)
                if g == 0:
                    wait(act, wo_full, i)
                act.activation(on_h[:, g, :], on[:], ACT.Copy).then_inc(onh_ok, 1)

            def m_evac(i, par):
                wait(act, mt_full, i + 1)
                wait(act, m_in, 16 * i)
                act.activation(mrow[:], ST_PS[0][0:HG * TB, 0:P], ACT.Copy, scale=-1.0).then_inc(mt_ok, 1)
                wait(act, mt_ok, i + 1)
                act.dma_start(qst[KS:KS + 1, par, :, :].bitcast(F32).rearrange(
                    "o h (t n) -> o (h t) n", t=TB), mrow[:].bitcast(F32)).then_inc(m_in, 16)

            def s_evac(b, t):
                n = 4 * b + t
                wait(act, wo_full, n + 1)
                act.activation(s_sb[:, t, :], W_PS[:], ACT.Copy).then_inc(s_ev, 1)
                wait(act, s_ev, n + 1)
                dst = s_dram[b, t * P:(t + 1) * P, :] if isinstance(b, int) else \
                    s_dram[bass.ds(b, 1), t * P:(t + 1) * P, :].rearrange("o p d -> (o p) d")
                act.dma_start(dst, s_sb[:, t, :]).then_inc(s_out[t % 2], 16)

            def beat(r, c):
                j, k = 16 * r + c, c % 4
                attend = there(j, NB)
                if there(j + 4, NB):
                    t_evac(j + 4, (c + 4) // 4 % 2, (c + 4) % 4)
                if k == 3 and there(4 * r + (c - 7) // 4, B * G):
                    o_high(4 * r + (c - 7) // 4, (c - 7) // 4 % 4)
                if c == 0 and isinstance(r, int) and r == 0:
                    act.wait_ge(w_lo, G + 1)
                if attend and k:
                    exps(j, c, 0)
                if there(j - 1, NB):
                    o_evac(j - 1, 4 * r + (c - 1) // 4, (c - 1) % 4)
                if there(j + 6, NB):
                    square(j + 6, (c + 6) % 2, (c + 6) // 4 % VR, (c + 6) % 4)
                if attend and k == 0:
                    exps(j, c, 0)
                d, t = at(c, 9)
                if t is not None and there(r + 1 + d, B):
                    xt_high(r + 1 + d, t)
                if attend:
                    exps(j, c, 1)
                if there(j + 5, NB):
                    t_high(j + 5, (c + 5) % 2)
                if attend:
                    exps(j, c, 2)
                d, t = at(c, 19)
                if t is not None and there(r + d, B):
                    s_evac(r + d, t)
                if k == 3 and there(j + 4, NB):
                    m_evac(4 * r + (c + 4) // 4, (c + 4) // 4 % 2)
                if isinstance(r, int) and r == 0 and -6 <= c <= -3:
                    split_w(c + 7)

            split_w(0)
            run_beats(act, beat)
            act.sem_inc(a_act, 1)

            act.wait_ge(c2_in, 48)

            def gate(b, m):
                n = MT * b + m
                wait(act, gu_full, n + 1)
                wait_slot(act, hf_ok, n, m)
                act.activation(gs[:, GP(m), :], GU_PS[2 * GP(m)][:], ACT.Silu,
                               scale=sgu[:, 0, m:m + 1]).then_inc(gs_ok, 1)

            def high(b, m):
                n = MT * b + m
                wait(act, hf_ok, n + 1)
                if m == 0:
                    wait(act, dn_full, 4 * b)
                act.activation(ht_h[:, m, :], hf[:, GP(m), :], ACT.Copy).then_inc(hh_ok, 1)

            def outer(b, t):
                n = 4 * b + t
                wait(act, y_ok, n + 1)
                wait_slot(act, sgx_ok, n, t)
                act.activation(gt[:, t % 2, :], yt[:, t % 2, :], ACT.Silu).then_inc(g_ok, 1)

            odd = [0]

            def GP(m):
                return (m + odd[0]) % 2

            with act.Fori(0, B // 2) as bb:
                for e in range(2):
                    odd[0] = e * MT % 2
                    b = 2 * bb + e
                    for m in range(MT):
                        gate(b, m)
                        if m:
                            high(b, m - 1)
                    high(b, MT - 1)
                    for t in range(TB):
                        outer(b, t)

        @block.vector
        def _(dve):
            dve.wait_ge(c_in, 16 * 8)
            dve.tensor_copy(idr[:], idf[:]).then_inc(idr_ok, 1)

            def split_w(g):
                dve.wait_ge(w_hi, g + 1)
                if g < G:
                    cols = slice(g * 3 * GC, (g + 1) * 3 * GC)
                    dve.tensor_tensor(wq_l[:, :, cols], stage[:, :, cols], wq_h[:, :, cols].bitcast(F32),
                                      ALU.subtract).then_inc(w_lo, 1)
                else:
                    dve.tensor_tensor(wo_l[:], stage[:, :, G * 3 * GC:], wo_h[:].bitcast(F32),
                                      ALU.subtract).then_inc(w_lo, 1)

            def ln_stats(b, t):
                n = 4 * b + t
                s = t % 2
                wait(dve, x_in[t], 16 * (b + 1))
                dve.bn_stats(st6[:, s, 0:6], xr[:, t, :]).then_inc(ln_s, 1)
                wait(dve, ln_s, n + 1)
                dve.tensor_copy(st6[:, s, 6:7], st6[:, s, 0:1])
                dve.bn_aggr(mv[:, s, 0:2], st6[:, s, 0:6]).then_inc(ln_a, 1)
                wait(dve, ln_a, n + 1)
                dve.tensor_scalar(ve[:, s, 0:1], mv[:, s, 1:2], LN_EPS, None, ALU.add).then_inc(ln_v, 1)

            def ln_apply(b, t):
                n = 4 * b + t
                s = t % 2
                wait(dve, ln_r, n + 1)
                dve.tensor_scalar(xr[:, t, :], xr[:, t, :], mv[:, s, 0:1], rstd[:, s, 0:1],
                                  ALU.subtract, ALU.mult).then_inc(xn_ok, 1)

            def xt_low(b, t):
                n = 4 * b + t
                wait(dve, xt_hi, n + 1)
                cols = slice(t * P, (t + 1) * P)
                dve.tensor_tensor(xnt_l[:, :, cols], W_PS[:].rearrange("p (k n) -> p k n", k=KT),
                                  xnt_h[:, :, cols].bitcast(F32), ALU.subtract).then_inc(xt_lo, 1)

            def squares(n, s):
                wait(dve, sq_ok, n + 1)
                wait(dve, rr_ok, n - 1)
                dve.tensor_reduce(ss[:, s, :], sq[:, s], AX.X, ALU.add).then_inc(ss_ok, 1)

            def unit_rms(n, s, v, t):
                wait(dve, rr_ok, n + 1)
                wait(dve, rope_ok, n - 1)
                wait(dve, vh_ok, n + 1)
                dve.tensor_tensor(qn[:, s].rearrange("p a h d -> p (a h) d"),
                                  QKV_PS[s][:, 0:2 * GC].rearrange("p (h d) -> p h d", d=HD),
                                  rr[:, s, :].rearrange("p (h o) -> p h o", o=1).to_broadcast([P, 2 * HG, HD]),
                                  ALU.mult).then_inc(qn_ok, 1)
                dve.tensor_tensor(va[:, v, t, :, HD:2 * HD],
                                  QKV_PS[s][:, 2 * GC:3 * GC].rearrange("p (h d) -> p h d", d=HD),
                                  va[:, v, t, :, 0:HD].bitcast(F32), ALU.subtract).then_inc(vl_ok, 1)

            def rope_sum(n, s):
                wait(dve, rope_ok, n + 1)
                wait(dve, tl_ok, n - 1)
                wait(dve, th_ok, n - 1)
                dve.tensor_tensor(qp[:, s, :], ra[:, s].rearrange("p a h d -> p (a h d)"),
                                  rb[:, s].rearrange("p a h d -> p (a h d)"), ALU.add).then_inc(qp_ok, 1)

            def t_low(n, s):
                wait(dve, th_ok, n + 1)
                dve.tensor_tensor(tt[:, s, :, 2:5:2, :], qp[:, s, :].rearrange("p (a h d) -> p h a d", a=2, h=HG),
                                  tt[:, s, :, 0:4:3, :].bitcast(F32), ALU.subtract).then_inc(tl_ok, 1)

            def p_low(j, e):
                w = sum(o[2] for o in ST_OPS[e])
                wait(dve, p_ok, NOP * j + e + 1)
                dve.tensor_tensor(pl[:, e, 0:w], pf[:, e, 0:w], ph[:, e, 0:w].bitcast(F32),
                                  ALU.subtract).then_inc(pl_ok, 1)

            def maxima(r, c, ops):
                qb, w = c % 4, (c % 4 + 1) * P
                for o in ops:
                    if o >= len(SM_OPS[qb]):
                        continue
                    heads = SM_OPS[qb][o]
                    if qb == 0 and o == 0:
                        wait(dve, mt_full, 4 * r + c // 4)
                    wait(dve, sm_full, sm_count(r, c) + o + 1)
                    h0 = heads[0]
                    dve.tensor_reduce(mx[:].rearrange("p (h t) -> p h t", t=TB)[:, h0:h0 + len(heads), qb],
                                      X_PS[(sm_count(0, c) + o) % 2][:, 0:len(heads) * w].rearrange(
                                          "p (h n) -> p h n", n=w), AX.X, ALU.max).then_inc(sm_ok, 1)

            def recip(i):
                wait(dve, d_in, 16 * (i + 1))
                wait(dve, rd_out, 16 * i)
                dve.reciprocal(rd16[:], den16[:]).then_inc(rd_ok, 1)

            def o_low(i, g):
                wait(dve, onh_ok, i + 1)
                dve.tensor_tensor(on_l[:, g, :], on[:], on_h[:, g, :].bitcast(F32),
                                  ALU.subtract).then_inc(onl_ok, 1)

            def beat(r, c):
                j, k = 16 * r + c, c % 4
                attend, mxs = there(j, NB), there(j + 4, NB)
                d, t = at(c, 9)
                if t is not None and there(r + 1 + d, B):
                    ln_apply(r + 1 + d, t)
                if there(j + 5, NB):
                    unit_rms(j + 5, (c + 5) % 2, (c + 5) // 4 % VR, (c + 5) % 4)
                if mxs:
                    maxima(r, c + 4, (0, 1) if k > 1 else (0,))
                if t is not None and there(r + 1 + d, B):
                    xt_low(r + 1 + d, t)
                if attend and k:
                    p_low(j, 0)
                if there(j + 6, NB):
                    squares(j + 6, (c + 6) % 2)
                if attend and k == 0:
                    p_low(j, 0)
                if there(j + 5, NB):
                    rope_sum(j + 5, (c + 5) % 2)
                if mxs:
                    maxima(r, c + 4, (2,) if k > 1 else (1,))
                if attend:
                    p_low(j, 1)
                if k == 3 and there(4 * r + (c - 7) // 4, B * G):
                    o_low(4 * r + (c - 7) // 4, (c - 7) // 4 % 4)
                if mxs and k > 1:
                    maxima(r, c + 4, (3,))
                if there(j + 5, NB):
                    t_low(j + 5, (c + 5) % 2)
                if attend:
                    p_low(j, 2)
                if k == 1 and there(4 * r + (c - 5) // 4, B * G):
                    recip(4 * r + (c - 5) // 4)
                d, t = at(c, 8)
                if t is not None and there(r + 1 + d, B):
                    ln_stats(r + 1 + d, t)
                if isinstance(r, int) and r == 0 and -6 <= c <= -3:
                    split_w(c + 7)

            split_w(0)
            run_beats(dve, beat)
            dve.sem_inc(a_dve, 1)

            dve.wait_ge(a_act, 1)
            dve.wait_ge(a_pool, 1)
            dve.wait_ge(wo_full, 4 * B)
            dve.wait_ge(xs_out, 32 * B)
            for m in range(MT):
                dve.wait_ge(ws_in[m % 2], 16 * (m // 2 + 1))
                dve.tensor_scalar(wgu[:, m], wst[:, m % 2, :].rearrange("p (k n) -> p k n", k=KT), -ZERO, None,
                                  ALU.add).then_inc(wc_ok, 1)

            def down_weights():
                for q in range(MT):
                    n = MT + q
                    dve.wait_ge(ws_in[n % 2], 16 * (n // 2 + 1))
                    dve.tensor_scalar(wd[:, q, :], wst[:, n % 2, 0:H], -ZERO, None, ALU.add).then_inc(wc_ok, 1)

            def hidden(b, m, s):
                n = MT * b + m
                wait(dve, gs_ok, n + 1)
                wait_slot(dve, hh_ok, n, m)
                wait_slot(dve, hl_ok, n, m)
                dve.scalar_tensor_tensor(hf[:, s, :], GU_PS[2 * s + 1][:], sgu[:, 1, m:m + 1], gs[:, s, :],
                                         ALU.mult, ALU.mult).then_inc(hf_ok, 1)

            def low(b, m, s):
                n = MT * b + m
                wait(dve, hh_ok, n + 1)
                dve.tensor_tensor(ht_l[:, m, :], hf[:, s, :], ht_h[:, m, :].bitcast(F32),
                                  ALU.subtract).then_inc(hl_ok, 1)

            def scaled(b, t):
                n = 4 * b + t
                wait(dve, dn_full, n + 1)
                wait_slot(dve, g_ok, n, t)
                dve.tensor_tensor(yt[:, t % 2, :], DN_PS[t][:], sdb[:], ALU.mult).then_inc(y_ok, 1)

            def finish(b, t):
                n = 4 * b + t
                s = t % 2
                wait(dve, g_ok, n + 1)
                wait(dve, xs_in[s], 32 * (2 * b + t // 2 + 1))
                wait(dve, r_out[s], 16 * (2 * b + t // 2))
                dve.tensor_tensor(res[:, s, :], gt[:, s, :], xs[:, s, 1, :], ALU.mult).then_inc(sgx_ok, 1)
                wait(dve, sgx_ok, n + 1)
                dve.tensor_tensor(res[:, s, :], res[:, s, :], xs[:, s, 0, :], ALU.add).then_inc(res_ok, 1)

            dve.wait_ge(c2_in, 48)
            down_weights()
            with dve.Fori(0, B // 2) as bb:
                for e in range(2):
                    b = 2 * bb + e
                    for m in range(MT):
                        s = (m + e * MT) % 2
                        hidden(b, m, s)
                        if m:
                            low(b, m - 1, 1 - s)
                    low(b, MT - 1, s)
                    for t in range(TB):
                        scaled(b, t)
                        if t:
                            finish(b, t - 1)
                    finish(b, TB - 1)

        @block.tensor
        def _(pe):
            pe.wait_ge(c_in, 16 * 8)
            pe.wait_ge(idr_ok, 1)
            pe.wait_ge(ones_ok, 4)

            def xn_turn(b, t):
                n = 4 * b + t
                wait(pe, xn_ok, n + 1)
                wait(pe, xt_lo, n)
                wait(pe, s_ev, 4 * (b - 1))
                for k in range(KT):
                    op = pe.transpose(W_PS[:, k * P:(k + 1) * P], xr[:, t, k * P:(k + 1) * P], idf[:])
                op.then_inc(xt_full, 1)

            def project(r, c, half_):
                n, g, t, s = 16 * r + c, c // 4 % 4, c % 4, c % 2
                if half_ == 0:
                    if g == 0:
                        b = r + c // 16
                        wait(pe, xt_hi, 4 * b + t + 1)
                        wait(pe, xt_lo, 4 * b + t + 1)
                    if isinstance(n, int) and n < 16:
                        pe.wait_ge(w_lo, g + 1)
                    wait(pe, sq_ok, n - 1)
                    wait(pe, vh_ok, n - 1)
                    wait(pe, vl_ok, n - 1)
                cols = slice(g * 3 * GC, (g + 1) * 3 * GC)
                todo = [(x_, w_, k) for x_, w_ in ((xnt_h, wq_h), (xnt_l, wq_h), (xnt_h, wq_l)) for k in range(KT)]
                m = len(todo) // 2
                for a, (x_, w_, k) in list(enumerate(todo))[half_ * m:half_ * m + m]:
                    op = pe.matmul(QKV_PS[s][:, 0:3 * GC], x_[:, k, t * P:(t + 1) * P], w_[:, k, cols],
                                   start=(a == 0), stop=(a == len(todo) - 1))
                if half_:
                    op.then_inc(qkv_full, 1)

            def turn(r, c):
                n, s = 16 * r + c, c % 2
                wait(pe, tl_ok, n + 1)
                wait(pe, sm_ok, sm_count(r, c))
                for a, full in ((0, tq_full), (1, tk_full)):
                    for h in range(HG):
                        op = pe.transpose(X_PS[a][0:KS, h * P:(h + 1) * P].bitcast(F32R),
                                          tt[:, s, h, 3 * a:3 * a + 3, :].rearrange("p c d -> p (c d)"), idr[:])
                    op.then_inc(full, 1)

            def scores_t(r, c, e):
                n, par, h = NOP * (16 * r + c) + e, c // 4 % 2, c % 4
                if h == 0 and e == 0:
                    wait(pe, m_in, 16 * (4 * r + c // 4 + 1))
                wait(pe, p_ok, n - 1)
                bank = ST_PS[(NOP * c + e) % 2]
                for j, c0, w in ST_OPS[e]:
                    pe.matmul(bank[:, c0:c0 + w], kst[0:KS + 1, par, h, j * P:(j + 1) * P],
                              qst[0:KS + 1, par, h, j * P:N], start=True, stop=False)
                    op = pe.matmul(bank[:, c0:c0 + P], idb[:], msk_t[:], start=False, stop=True)
                op.then_inc(st_full, 1)

            def p_v(r, c, e):
                j_, v, h = 16 * r + c, c // 4 % VR, c % 4
                wait(pe, pl_ok, NOP * j_ + e + 1)
                if e == 0:
                    wait(pe, o_ev, j_)
                    if h == 0:
                        wait(pe, vl_ok, j_ + 4)
                for j, c0, w in ST_OPS[e]:
                    for part in (ph, pl):
                        op = pe.matmul(PV_PS[0:VW, j * P:N], va[:, v, j, h, :], part[:, e, c0:c0 + w],
                                       start=(j == 0 and part is ph), stop=(j == 2 and part is pl))
                op.then_inc(pv_ok, 1)

            def maxima(r, c, ops):
                n, par, qb, w = 16 * r + c, c // 4 % 2, c % 4, (c % 4 + 1) * P
                for o in ops:
                    if o >= len(SM_OPS[qb]):
                        continue
                    if o == 0:
                        wait(pe, tq_ev, n + 1)
                        wait(pe, tk_ev, n + 1)
                    wait(pe, sm_ok, sm_count(r, c) + o - 1)
                    bank = X_PS[(sm_count(0, c) + o) % 2]
                    for a, h in enumerate(SM_OPS[qb][o]):
                        pe.matmul(bank[:, a * w:(a + 1) * w], qst[0:KS, par, h, qb * P:(qb + 1) * P],
                                  kst[0:KS, par, h, 0:w], start=True, stop=False)
                        op = pe.matmul(bank[:, (a + 1) * w - P:(a + 1) * w], idb[:], msk_s[:], start=False, stop=True)
                    op.then_inc(sm_full, 1)

            def max_turn(r, c):
                wait(pe, sm_ok, sm_count(r, c + 1))
                wait(pe, p_ok, NOP * (16 * r + c - 4) + 2)
                pe.transpose(ST_PS[0][0:HG * TB, 0:P], mx[:], idf[:]).then_inc(mt_full, 1)

            def out_proj(b, t):
                n = 4 * b + t
                if t == 0:
                    wait(pe, onl_ok, 4 * b + 4)
                    wait(pe, xt_lo, 4 * min(b + 2, B) if isinstance(b, int) else 4 * (b + 2))
                    pe.wait_ge(w_lo, G + 1)
                wait(pe, s_ev, n)
                todo = [(o_, w_, g) for o_, w_ in ((on_h, wo_h), (on_l, wo_h), (on_h, wo_l)) for g in range(G)]
                for j, (o_, w_, g) in enumerate(todo):
                    op = pe.matmul(W_PS[:], o_[:, g, t * P:(t + 1) * P], w_[:, g, :],
                                   start=(j == 0), stop=(j == len(todo) - 1))
                op.then_inc(wo_full, 1)

            def beat(r, c):
                j, k = 16 * r + c, c % 4
                attend, mxs, proj = there(j, NB), there(j + 4, NB), there(j + 6, NB)
                if attend and k:
                    scores_t(r, c, 0)
                if proj:
                    project(r, c + 6, 0)
                if mxs:
                    maxima(r, c + 4, (0, 1) if k > 1 else (0,))
                if attend and k:
                    scores_t(r, c, 1)
                if proj:
                    project(r, c + 6, 1)
                if attend and k == 0:
                    scores_t(r, c, 0)
                    scores_t(r, c, 1)
                if mxs:
                    maxima(r, c + 4, (2,) if k > 1 else (1,))
                d, t = at(c, 9)
                if t is not None and there(r + 1 + d, B):
                    xn_turn(r + 1 + d, t)
                if attend:
                    p_v(r, c, 0)
                    scores_t(r, c, 2)
                if mxs and k > 1:
                    maxima(r, c + 4, (3,))
                if attend:
                    p_v(r, c, 1)
                if k == 3 and mxs:
                    max_turn(r, c + 4)
                if there(j + 5, NB):
                    turn(r, c + 5)
                if attend:
                    p_v(r, c, 2)
                d, t = at(c, 19)
                if t is not None and there(r + d, B):
                    out_proj(r + d, t)

            run_beats(pe, beat)
            pe.wait_ge(s_ev, 4 * B)

            def gate_up(b, par, m, s):
                n = MT * b + m
                wait(pe, wc_ok, m + 1)
                wait_slot(pe, hf_ok, n, m)
                for a in range(2):
                    todo = [(x_, k) for x_ in (xb_h, xb_l) for k in range(KT)]
                    for j, (x_, k) in enumerate(todo):
                        op = pe.matmul(GU_PS[2 * s + a][:], wgu[:, m, k, a * P:(a + 1) * P], x_[:, par, k, :],
                                       start=(j == 0), stop=(j == len(todo) - 1))
                op.then_inc(gu_full, 1)

            def down(b, t):
                n = 4 * b + t
                wait_slot(pe, y_ok, n, t, TB)
                if t == 0:
                    pe.wait_ge(wc_ok, 2 * MT)
                for m in range(MT):
                    if t == 0:
                        wait(pe, hl_ok, MT * b + m + 1)
                    for h_ in (ht_h, ht_l):
                        op = pe.matmul(DN_PS[t][:], h_[:, m, t * P:(t + 1) * P], wd[:, m, :],
                                       start=(m == 0 and h_ is ht_h), stop=(m == MT - 1 and h_ is ht_l))
                op.then_inc(dn_full, 1)

            with pe.Fori(0, B // 2) as bb:
                for e in range(2):
                    b = 2 * bb + e
                    wait(pe, xb_in[e], 32 * (bb + 1))
                    for m in range(MT):
                        gate_up(b, e, m, (m + e * MT) % 2)
                    for t in range(TB):
                        down(b, t)


def kernel(L0_attn_x, L0_attn_w_qkv, L0_attn_w_out, L0_attn_q_gamma, L0_attn_k_gamma,
           L0_ffn_wq_gate, L0_ffn_s_gate, L0_ffn_wq_up, L0_ffn_s_up, L0_ffn_wq_down, L0_ffn_s_down):
    import ml_dtypes
    import concourse.bacc as bacc
    from concourse.bass_utils import run_bass_kernel_spmd

    def ar(a):
        return np.asarray(a)

    inv = (1.0 / np.float32(THETA) ** (np.arange(0, HD, 2, dtype=np.float32) / np.float32(HD))).astype(np.float32)
    ang = np.arange(N, dtype=np.float32)[:, None] * inv[None, :]
    ang = np.concatenate([ang, ang], -1)
    sign = np.where(np.arange(HD) < HD // 2, -1.0, 1.0)
    root = np.sqrt(float(HD))
    cos_tab = (np.cos(ang.astype(np.float64)) * root).astype(np.float32)
    sin_tab = (np.sin(ang.astype(np.float64)) * sign * root).astype(np.float32)
    tri = np.arange(P)
    arrays = {
        "x": np.ascontiguousarray(ar(L0_attn_x)),
        "w_qkv": np.ascontiguousarray(ar(L0_attn_w_qkv).reshape(KT, P, 3, G, GC).transpose(1, 0, 3, 2, 4)
                                      .reshape(P, KT, G * 3 * GC)),
        "w_out": np.ascontiguousarray(ar(L0_attn_w_out).reshape(KT, P, H).transpose(1, 0, 2)),
        "q_gamma": ar(L0_attn_q_gamma).reshape(1, HD),
        "k_gamma": ar(L0_attn_k_gamma).reshape(1, HD),
        "w_gu": np.ascontiguousarray(np.stack([ar(w).reshape(MT, P, KT, P).transpose(0, 3, 2, 1)
                                               for w in (L0_ffn_wq_gate, L0_ffn_wq_up)], 3).reshape(MT, P, KT, 2 * P)),
        "s_gate": np.ascontiguousarray(ar(L0_ffn_s_gate).reshape(MT, P).T),
        "s_up": np.ascontiguousarray(ar(L0_ffn_s_up).reshape(MT, P).T),
        "w_down": np.ascontiguousarray(ar(L0_ffn_wq_down).T.reshape(MT, P, H)),
        "s_down": ar(L0_ffn_s_down).reshape(1, H),
        "cos_tab": np.ascontiguousarray(cos_tab.reshape(TB, P, HD).transpose(1, 0, 2)),
        "sin_tab": np.ascontiguousarray(sin_tab.reshape(TB, P, HD).transpose(1, 0, 2)),
        "ident": np.eye(P, dtype=np.float32),
        "ident_b": np.eye(P, dtype=np.float32).astype(ml_dtypes.bfloat16),
        "mask_s": np.where(tri[None, :] > tri[:, None], NEG, 0.0).astype(ml_dtypes.bfloat16),
        "mask_t": np.where(tri[:, None] > tri[None, :], NEG, 0.0).astype(ml_dtypes.bfloat16),
    }
    nc = bacc.Bacc("TRN2", target_bir_lowering=False, num_devices=1)
    d = {k: nc.dram_tensor(k, a.shape, mybir.dt.from_np(a.dtype), kind="ExternalInput").ap()
         for k, a in arrays.items()}
    s_dram = nc.dram_tensor("s_dram", (B, N, H), F32, kind="Internal").ap()
    rd_dram = nc.dram_tensor("rd_dram", (1, HG * N), F32, kind="Internal").ap()
    xnt_dram = nc.dram_tensor("xnt_dram", (2, B, P, KT, N), F32, kind="Internal").ap()
    out = nc.dram_tensor("out", (B, N, H), F32, kind="ExternalOutput").ap()
    build(nc, d["x"], d["w_qkv"], d["w_out"], d["q_gamma"], d["k_gamma"], d["w_gu"], d["s_gate"], None,
          d["s_up"], d["w_down"], d["s_down"], d["cos_tab"], d["sin_tab"], d["ident"], d["ident_b"],
          d["mask_s"], d["mask_t"], s_dram, rd_dram, xnt_dram, out)
    r = run_bass_kernel_spmd(nc, [arrays], core_ids=[0])
    return r.results[0]["out"]
```

```python
from contextlib import ExitStack

import numpy as np

import concourse.bass as bass
from concourse import mybir

ALU = mybir.AluOpType
ACT = mybir.ActivationFunctionType
AX = mybir.AxisListType
F32 = mybir.dt.float32
F32R = mybir.dt.float32r
BF16 = mybir.dt.bfloat16
I32 = mybir.dt.int32

B, N, H = 4, 512, 512
NH = 16
HD = H // NH
P = 128
TB = N // P
KT = H // P
G = 4
HG = NH // G
GC = HG * HD
HID = 1408
MT = HID // P
LN_EPS, RMS_EPS, THETA, NEG, ZERO = 1e-5, 1e-6, 10000.0, -1e30, 128.0
SCALE = 1.0 / float(np.sqrt(HD))
VW = 2 * HD + 1
KS = 3 * HD
VR = 4
ST_OPS = [[(0, 0, 512)], [(1, 0, 384), (3, 384, 128)], [(2, 0, 256)]]
TURN = ()
SM_OPS = [[(0, 1, 2, 3)], [(0, 1), (2, 3)], [(0,), (1,), (2,), (3,)], [(0,), (1,), TURN, (2,), (3,)]]
SM_BASE = [sum(len(o) for o in SM_OPS[:t]) for t in range(TB)]
SM_UNIT = sum(len(o) for o in SM_OPS)
NOP = len(ST_OPS)
ST_W = [sum(o[2] for o in ops) for ops in ST_OPS]
ST_AT = [sum(ST_W[:e]) for e in range(NOP)]
UO = HG * NOP


def wait(eng, sem, value):
    if isinstance(value, int) and value <= 0:
        return
    eng.wait_ge(sem, value)


def wait_slot(eng, sem, n, pos, ring=2):
    value = n - pos if pos < ring - 1 else n - ring + 1
    if isinstance(value, int) and value <= 0:
        return
    eng.wait_ge(sem, value)


def build(nc, x, w_qkv, w_out, q_gamma, k_gamma, w_gate, s_gate, w_up, s_up, w_down, s_down,
          cos_tab, sin_tab, ident, ident_b, mask_s, mask_t, s_dram, rd_dram, xnt_dram, out):
    top = ExitStack()
    with top:
        def sem(name):
            return top.enter_context(nc.semaphore(name))

        def tiles(stack):
            def sb(name, shape, dt=F32):
                return stack.enter_context(nc.sbuf_tensor(name, shape, dt))
            return sb

        psum = [top.enter_context(nc.psum_tensor(f"bank{n}", [P, 512], F32)) for n in range(8)]
        QKV_PS, X_PS, W_PS, ST_PS, PV_PS = psum[0:2], psum[2:4], psum[4], psum[5:7], psum[7]
        GU_PS, DN_PS = psum[0:4], psum[4:8]

        pa = ExitStack()
        sb = tiles(pa)
        wq_h = sb("wq_h", [P, KT, G * 3 * GC], F32R)
        wq_l = sb("wq_l", [P, KT, G * 3 * GC], F32R)
        wo_h = sb("wo_h", [P, KT, H], F32R)
        wo_l = sb("wo_l", [P, KT, H], F32R)
        xnt_h = sb("xnt_h", [P, KT, N], F32R)
        xnt_l = sb("xnt_l", [P, KT, N], F32R)
        xr = sb("xr", [P, TB, H])
        with ExitStack() as early:
            stage = tiles(early)("stage", [P, KT, G * 3 * GC + H])
        on_h = sb("on_h", [P, G, N], F32R)
        on_l = sb("on_l", [P, G, N], F32R)
        oh = sb("oh", [P, N])
        ol = sb("ol", [P, N])
        rdb = sb("rdb", [P, N])
        on = sb("on", [P, N])
        oraw = sb("oraw", [VW, HG, N])
        s_sb = sb("s_sb", [P, 2, H])
        den16 = sb("den16", [P, HG * TB])
        rd16 = sb("rd16", [P, HG * TB])
        idf = sb("idf", [P, P])
        idr = sb("idr", [P, P], F32R)
        idb = sb("idb", [P, P], BF16)
        msk_s = sb("msk_s", [P, P], BF16)
        msk_t = sb("msk_t", [P, P], BF16)
        gam = sb("gam", [P, 2, HD])
        cg = sb("cg", [P, TB, 2, HD])
        sg = sb("sg", [P, TB, 2, HD])
        half = sb("half", [P, 8])

        st6 = sb("st6", [P, 2, 8])
        mv = sb("mv", [P, 2, 8])
        ve = sb("ve", [P, 2, 8])
        rstd = sb("rstd", [P, 2, 8])
        sq = sb("sq", [P, 2, 2 * HG, HD + 1])
        ss = sb("ss", [P, 2, 8])
        rr = sb("rr", [P, 2, 8])
        qn = sb("qn", [P, 2, 2, HG, HD])
        ra = sb("ra", [P, 1, 2, HG, HD])
        rb = sb("rb", [P, 1, 2, HG, HD])
        ctab, stab = rb[:, 0, 0], rb[:, 0, 1]
        qp = sb("qp", [P, 2, 2 * GC])
        tt = sb("tt", [P, 2, HG, 6, HD], F32R)
        qst = sb("qst", [P, 2, HG, N], F32R)
        kst = sb("kst", [P, 2, HG, N], F32R)
        va = sb("va", [P, VR, TB, HG, VW], F32R)
        mx = sb("mx", [P, HG * TB])
        mrow0 = sb("mrow0", [TB, P], F32R)
        mrow = sb("mrow", [(HG - 1) * TB, P], F32R)
        pf = sb("pf", [P, sum(ST_W)])
        ph = sb("ph", [P, sum(ST_W)], F32R)
        pl = sb("pl", [P, sum(ST_W)], F32R)
        pa.close()

        pbs = ExitStack()
        sb = tiles(pbs)
        wgu = sb("wgu", [P, MT, KT, 2 * P], F32R)
        scales = sb("scales", [P, 2 * KT * G * 3 * GC - MT * KT * 2 * P])
        sgu = scales[:, 0:2 * MT].rearrange("p (a m) -> p a m", a=2)
        sdb = scales[:, 2 * MT:2 * MT + H]
        yt = sb("yt", [P, 2, H])
        gt = sb("gt", [P, 2, H])
        res = sb("res", [P, 2, H])
        spare = sb("spare", [P, 2, H])
        held = sb("held", [P, 2 * KT * N + TB * H])
        xs = sb("xs", [P, TB, 2, H])
        held2 = sb("held2", [P, 4 * N + HG * N + 2 * H + 2 * HG * TB])
        wd = sb("wd", [P, MT, H], F32R)
        ht_h = sb("ht_h", [P, MT, N], F32R)
        ht_l = sb("ht_l", [P, MT, N], F32R)
        gs = sb("gs", [P, 2, N])
        hf = sb("hf", [P, 2, N])
        pbs.close()

        id_in, c_in = sem("id_in"), sem("c_in")
        w_in = [sem(f"w_in{g}") for g in range(G + 1)]
        w_hi, w_lo = sem("w_hi"), sem("w_lo")
        idr_ok, ones_ok, tab_c, tab_ok = sem("idr_ok"), sem("ones_ok"), sem("tab_c"), sem("tab_ok")
        x_in = [sem(f"x_in{t}") for t in range(TB)]
        ln_s, ln_a, ln_v, ln_r = sem("ln_s"), sem("ln_a"), sem("ln_v"), sem("ln_r")
        xn_ok, xt_full, xt_hi, xt_lo = sem("xn_ok"), sem("xt_full"), sem("xt_hi"), sem("xt_lo")
        xs_out = sem("xs_out")
        qkv_full, sq_ok, vh_ok, ss_ok, rr_ok = (sem(n) for n in ("qkv_full", "sq_ok", "vh_ok", "ss_ok", "rr_ok"))
        qn_ok, vl_ok, rope_ok, qp_ok = (sem(n) for n in ("qn_ok", "vl_ok", "rope_ok", "qp_ok"))
        th_ok, tl_ok, tq_full, tk_full = (sem(n) for n in ("th_ok", "tl_ok", "tq_full", "tk_full"))
        tq_ev, tk_ev = sem("tq_ev"), sem("tk_ev")
        sm_full, sm_ok, mt_full, mt_ok, m_in = (sem(n) for n in ("sm_full", "sm_ok", "mt_full", "mt_ok", "m_in"))
        m0_in = sem("m0_in")
        st_full, p_ok, pl_ok, pv_ok, o_ev = (sem(n) for n in ("st_full", "p_ok", "pl_ok", "pv_ok", "o_ev"))
        og_in, d_in, rd_ok, rd_out, rb_in = (sem(n) for n in ("og_in", "d_in", "rd_ok", "rd_out", "rb_in"))
        os_ok, on_ok, onh_ok, onl_ok = (sem(n) for n in ("os_ok", "on_ok", "onh_ok", "onl_ok"))
        wo_full, s_ev = sem("wo_full"), sem("s_ev")
        s_out = [sem("s_out0"), sem("s_out1")]
        ws_in = [sem("ws_in0"), sem("ws_in1")]
        wc_ok, wd_ok, c2_in, xb_in = sem("wc_ok"), sem("wd_ok"), sem("c2_in"), sem("xb_in")
        gu_full, gs_ok, hf_ok, hh_ok, hl_ok = (sem(n) for n in ("gu_full", "gs_ok", "hf_ok", "hh_ok", "hl_ok"))
        dn_full, y_ok, g_ok, sgx_ok, res_ok = (sem(n) for n in ("dn_full", "y_ok", "g_ok", "sgx_ok", "res_ok"))
        xs_in = [sem(f"xs_in{t}") for t in range(TB)]
        r_out = [sem("r_out0"), sem("r_out1")]

        block = top.enter_context(nc.Block())

        def run_beats(eng, beat):
            for c in range(-8, 12):
                beat(0, c)
            with eng.Fori(0, B - 2) as r:
                for c in range(12, 28):
                    beat(r, c)
            for c in range(-4, 17):
                beat(B - 1, c)

        LAST = B * G - 1
        O_HIGH, O_PROJ = 4, 5

        SPLIT_AT = (-8, -6, -5, -4, -3)
        STORE_AT = (2, 4, 7, 10)
        EARLY = 7

        def there(index, count):
            return not isinstance(index, int) or 0 <= index < count

        SM_A, SM_B, SM_C = [(0,), (0,), (0,), (0, 1)], [(), (1,), (1,), (3,)], [(), (), (2, 3), (4,)]
        SM_T = [(), (), (), (2,)]
        NB = B * G * TB

        def at(c, first):
            d, t = divmod(c - first, 16)
            return (d, t) if t < TB else (0, None)

        def ln_at(r, c):
            if isinstance(r, int) and r == 0 and c < TB - 8:
                return 0, c + 8
            b, t = r + 1 + c // 16, c % 16 - 4
            t = t if 0 <= t < TB else None
            return (b, t) if there(b, B) else (b, None)

        def sm_count(r, c):
            return SM_UNIT * 4 * r + SM_UNIT * (c // 4) + SM_BASE[c % 4]

        def load_x(eng, b, t):
            eng.dma_start(xr[:, t, :], x[b, t * P:(t + 1) * P, :]
                          if isinstance(b, int) else
                          x[bass.ds(b, 1), t * P:(t + 1) * P, :].rearrange("o p d -> (o p) d")
                          ).then_inc(x_in[t], 16)

        @block.sync
        def _(sp):
            def load_w(g):
                sp.dma_start(stage[:, :, g * 3 * GC:(g + 1) * 3 * GC],
                             w_qkv[:, :, g * 3 * GC:(g + 1) * 3 * GC]).then_inc(w_in[g], 16)

            load_x(sp, 0, 0)
            load_w(0)
            sp.dma_start(idf[:], ident).then_inc(id_in, 16)
            load_x(sp, 0, 1)
            for dst, src in ((ctab, cos_tab), (stab, sin_tab), (gam[:, 0, :], q_gamma.to_broadcast([P, HD])),
                             (gam[:, 1, :], k_gamma.to_broadcast([P, HD])), (idb[:], ident_b),
                             (msk_s[:], mask_s), (msk_t[:], mask_t)):
                sp.dma_start(dst, src).then_inc(c_in, 16)
            load_x(sp, 0, 2)
            load_w(1)
            load_x(sp, 0, 3)
            for g in range(2, G):
                load_w(g)
            sp.dma_start(stage[:, :, G * 3 * GC:], w_out).then_inc(w_in[G], 16)

            def gather(i, h):
                wait(sp, o_ev, 4 * i + h + 1)
                wait(sp, os_ok, i)
                sp.dma_start(oh[HD * h:HD * h + HD, :], oraw[0:HD, h, :]).then_inc(og_in, 16)
                sp.dma_start(ol[HD * h:HD * h + HD, :], oraw[HD:2 * HD, h, :]).then_inc(og_in, 16)

            def den_out(i):
                wait(sp, rd_ok, i)
                sp.dma_start(den16[:], oraw[2 * HD:VW, :, :].rearrange("o h (a n) -> o (h a) n", n=HG * TB)
                             ).then_inc(d_in, 16)

            def den_in(i):
                wait(sp, rd_ok, i + 1)
                sp.dma_start(rd_dram[0:1, :].rearrange("o (p n) -> (o p) n", n=HG * TB),
                             rd16[:]).then_inc(rd_out, 16)
                wait(sp, rd_out, 16 * (i + 1))
                wait(sp, on_ok, i)
                sp.dma_start(rdb[:], rd_dram.rearrange("o (h n) -> (o h) n", h=HG).rearrange(
                    "h (o n) -> h o n", o=1).to_broadcast([HG, HD, N])).then_inc(rb_in, 16)

            def load_xb(b):
                for n, t in ((0, xnt_h), (1, xnt_l)):
                    src = xnt_dram[n, b] if isinstance(b, int) else \
                        xnt_dram[n, bass.ds(b, 1)].rearrange("o p k n -> (o p) k n")
                    sp.dma_start(t[:].bitcast(F32), src).then_inc(xb_in, 16)

            def load_gu(m):
                wait(sp, wc_ok, m - 1)
                sp.dma_start(xr[:, 2 * (m % 2):2 * (m % 2) + 2, :].bitcast(I32).rearrange("p a n -> p (a n)"),
                             w_gate[m].rearrange("p k n -> p (k n)")).then_inc(ws_in[m % 2], 16)

            def m0_out(r, c, par):
                wait(sp, sm_ok, sm_count(r, c) + 3)
                sp.dma_start(qst[KS:KS + 1, par, 0:1, :].bitcast(F32).rearrange(
                    "o h (t n) -> o (h t) n", t=TB), mrow0[:].bitcast(F32)).then_inc(m0_in, 16)

            def m_out(r, c, par):
                wait(sp, mt_ok, 4 * r + c // 4 + 1)
                sp.dma_start(qst[KS:KS + 1, par, 1:HG, :].bitcast(F32).rearrange(
                    "o h (t n) -> o (h t) n", t=TB), mrow[:].bitcast(F32)).then_inc(m_in, 16)

            def s_store(b, t):
                wait(sp, s_ev, 4 * b + t + 1)
                dst = s_dram[b, t * P:(t + 1) * P, :] if isinstance(b, int) else \
                    s_dram[bass.ds(b, 1), t * P:(t + 1) * P, :].rearrange("o p d -> (o p) d")
                sp.dma_start(dst, s_sb[:, t % 2, :]).then_inc(s_out[t % 2], 16)

            def beat(r, c):
                k, final = c % 4, isinstance(r, int) and r == B - 1
                if c % 16 == 12 and there(r + c // 16 + 2, B):
                    nb = r + c // 16 + 2
                    turned = sp.snap(4 * nb)
                    wait(sp, xt_full, turned)
                    for t in range(TB):
                        load_x(sp, nb, t)
                if final and c == 9:
                    wait(sp, qkv_full, NB)
                    sp.dma_start(sgu[:, 0, :], s_gate).then_inc(c2_in, 16)
                    sp.dma_start(sgu[:, 1, :], s_up).then_inc(c2_in, 16)
                    sp.dma_start(sdb[:], s_down.to_broadcast([P, H])).then_inc(c2_in, 16)
                if final and 0 <= c - 9 < EARLY:
                    load_gu(c - 9)
                if final and c == 12:
                    wait(sp, xs_out, 32 * B)
                    load_xb(0)
                if k == 3 and there(16 * r + c + 4, NB):
                    m0_out(r, c + 4, (c + 4) // 4 % 2)
                if k == 3 and there(16 * r + c - 1, NB):
                    gather(4 * r + (c - 1) // 4, (c - 1) % 4)
                if k == 3 and there(16 * r + c + 4, NB):
                    m_out(r, c + 4, (c + 4) // 4 % 2)
                d, t = at(c, 20)
                if t is not None and there(r + d, B):
                    s_store(r + d, t)
                if k != 3 and there(16 * r + c - 1, NB):
                    i, h = 4 * r + (c - 1) // 4, (c - 1) % 4
                    gather(i, h)
                    if h == HG - 1:
                        den_out(i)
                        den_in(i)
                d, t = at(c, 9)
                if t == TB - 1 and there(r + 1 + d, B):
                    nb = r + 1 + d
                    wait(sp, xt_hi, 4 * nb + 4)
                    wait(sp, xt_lo, 4 * nb + 4)
                    for n, t_ in ((0, xnt_h), (1, xnt_l)):
                        dst = xnt_dram[n, nb] if isinstance(nb, int) else \
                            xnt_dram[n, bass.ds(nb, 1)].rearrange("o p k n -> (o p) k n")
                        sp.dma_start(dst, t_[:].bitcast(F32)).then_inc(xs_out, 16)

            run_beats(sp, beat)
            for m in range(EARLY, MT):
                load_gu(m)
            for q in range(MT):
                n = MT + q
                if q in STORE_AT:
                    s_store(B - 1, STORE_AT.index(q))
                if q < 2:
                    sp.wait_ge(wc_ok, n - 1)
                else:
                    sp.wait_ge(wd_ok, q - 1)
                sp.dma_start(xr[:, 2 * (n % 2), :].bitcast(I32), w_down[q]).then_inc(ws_in[n % 2], 16)

            def load_xs(b, t):
                rows = slice(t * P, (t + 1) * P)
                for a, src in ((0, x), (1, s_dram)):
                    v = src[b, rows, :] if isinstance(b, int) else \
                        src[bass.ds(b, 1), rows, :].rearrange("o p d -> (o p) d")
                    sp.dma_start(xs[:, t, a, :], v).then_inc(xs_in[t], 16)

            def store(b, t):
                wait(sp, res_ok, 4 * b + t + 1)
                v = out[b, t * P:(t + 1) * P, :] if isinstance(b, int) else \
                    out[bass.ds(b, 1), t * P:(t + 1) * P, :].rearrange("o p d -> (o p) d")
                sp.dma_start(v, res[:, t % 2, :]).then_inc(r_out[t % 2], 16)

            sp.wait_ge(wo_full, 4 * B)
            sp.wait_ge(s_out[0], 16 * (2 * B + 1))
            sp.wait_ge(s_out[1], 16 * (2 * B + 1))
            for t in range(TB):
                load_xs(0, t)
            with sp.Fori(1, B) as b:
                wait(sp, gu_full, MT * b)
                load_xb(b)
                for t in range(TB):
                    store(b - 1, t)
                    load_xs(b, t)
            for t in range(TB):
                store(B - 1, t)
            for n in range(2):
                sp.wait_ge(r_out[n], 16 * 2 * B)

        @block.gpsimd
        def _(pool):
            pool.memset(kst[KS:KS + 1, :, :, :].bitcast(F32), 1.0).then_inc(ones_ok, 1)
            pool.wait_ge(ones_ok, 1)
            pool.memset(half[:], -0.5).then_inc(ones_ok, 1)
            pool.memset(sq[:, :, :, HD:HD + 1], HD * RMS_EPS).then_inc(ones_ok, 1)
            pool.memset(va[:, :, :, :, 2 * HD:VW].bitcast(F32), 1.0).then_inc(ones_ok, 1)
            pool.wait_ge(ones_ok, 4)

            def tables():
                pool.wait_ge(c_in, 16 * 7)
                for a in range(2):
                    for t in range(TB):
                        pool.tensor_tensor(cg[:, t, a, :], ctab[:, t, :], gam[:, a, :], ALU.mult).then_inc(tab_ok, 1)
                        for lo, hi in ((0, HD // 2), (HD // 2, 0)):
                            pool.tensor_tensor(sg[:, t, a, lo:lo + HD // 2], stab[:, t, lo:lo + HD // 2],
                                               gam[:, a, hi:hi + HD // 2], ALU.mult).then_inc(tab_ok, 1)
                pool.wait_ge(tab_ok, 2 * TB * 3)

            def rstd_block(b, t):
                n = 4 * b + t
                wait(pool, ln_v, n + 1)
                pool.tensor_tensor(rstd[:, t % 2, 0:1], ve[:, t % 2, 0:1], half[:, 0:1], ALU.pow).then_inc(ln_r, 1)

            def inv_rms(n, s):
                wait(pool, ss_ok, n + 1)
                pool.tensor_tensor(rr[:, s, :], ss[:, s, :], half[:], ALU.pow).then_inc(rr_ok, 1)

            def rope(n, s, t):
                wait(pool, qn_ok, n + 1)
                wait(pool, qp_ok, n)
                hh = HD // 2
                for a in range(2):
                    pool.tensor_tensor(ra[:, 0, a], qn[:, s, a],
                                       cg[:, t, a, :].rearrange("p (o d) -> p o d", o=1).to_broadcast([P, HG, HD]), ALU.mult)
                for a in range(2):
                    for lo, hi in ((0, hh), (hh, 0)):
                        op = pool.tensor_tensor(
                            rb[:, 0, a, :, lo:lo + hh], qn[:, s, a, :, hi:hi + hh],
                            sg[:, t, a, lo:lo + hh].rearrange("p (o d) -> p o d", o=1).to_broadcast([P, HG, hh]), ALU.mult)
                op.then_inc(rope_ok, 1)

            def out_sum(i):
                wait(pool, og_in, 16 * 2 * HG * (i + 1))
                wait(pool, onl_ok, i)
                pool.tensor_tensor(on[:], oh[:], ol[:], ALU.add).then_inc(os_ok, 1)

            def norm(i):
                wait(pool, os_ok, i + 1)
                wait(pool, rb_in, 16 * (i + 1))
                pool.tensor_tensor(on[:], on[:], rdb[:], ALU.mult).then_inc(on_ok, 1)

            def beat(r, c):
                j, k = 16 * r + c, c % 4
                if there(j + 6, NB):
                    inv_rms(j + 6, (c + 6) % 2)
                if there(j + 6, NB):
                    rope(j + 6, (c + 6) % 2, (c + 6) % 4)
                b, t = ln_at(r, c)
                if t is not None:
                    rstd_block(b, t)
                if isinstance(r, int) and r == 0 and c == -8:
                    tables()
                if k == 1 and there(4 * r + (c - 5) // 4, B * G):
                    out_sum(4 * r + (c - 5) // 4)
                if k == 2 and there(4 * r + (c - 6) // 4, B * G):
                    norm(4 * r + (c - 6) // 4)

            run_beats(pool, beat)
            out_sum(LAST)
            norm(LAST)
            pool.wait_ge(pv_ok, NOP * NB)
            for q in range(MT):
                n = MT + q
                count = len(range(n % 2, MT, 2)) + q // 2 + 1
                pool.wait_ge(ws_in[n % 2], 16 * count)
                pool.tensor_scalar(wd[:, q, :], xr[:, 2 * (n % 2), :].bitcast(I32), -ZERO, None, ALU.add).then_inc(wd_ok, 1)

        @block.scalar
        def _(act):
            def split_w(g):
                act.wait_ge(w_in[g], 16)
                if g < G:
                    cols = slice(g * 3 * GC, (g + 1) * 3 * GC)
                    act.activation(wq_h[:, :, cols], stage[:, :, cols], ACT.Copy).then_inc(w_hi, 1)
                else:
                    act.activation(wo_h[:], stage[:, :, G * 3 * GC:], ACT.Copy).then_inc(w_hi, 1)

            def xt_high(b, t):
                n = 4 * b + t
                wait(act, xt_full, n + 1)
                if t == 0:
                    wait(act, xs_out, 32 * b)
                wait(act, qkv_full, 4 * (4 * b - 1) + t + 1)
                act.activation(xnt_h[:, :, t * P:(t + 1) * P], W_PS[:].rearrange("p (k n) -> p k n", k=KT),
                               ACT.Copy).then_inc(xt_hi, 1)

            def square(n, s, v, t):
                wait(act, qkv_full, n + 1)
                wait(act, ss_ok, n - 1)
                act.activation(sq[:, s, :, 0:HD], QKV_PS[s][:, 0:2 * GC].rearrange("p (h d) -> p h d", d=HD),
                               ACT.Square).then_inc(sq_ok, 1)
                act.activation(va[:, v, t, :, 0:HD],
                               QKV_PS[s][:, 2 * GC:3 * GC].rearrange("p (h d) -> p h d", d=HD),
                               ACT.Copy).then_inc(vh_ok, 1)

            def t_high(n, s):
                wait(act, qp_ok, n + 1)
                wait(act, tk_full, n - 1)
                v = qp[:, s, :].rearrange("p (a h d) -> p h a d", a=2, h=HG)
                act.activation(tt[:, s, :, 0:4:3, :], v, ACT.Copy)
                act.activation(tt[:, s, :, 1:6:4, :], v, ACT.Copy).then_inc(th_ok, 1)

            def q_evac(n, par, t):
                if t == 0:
                    wait(act, st_full, NOP * (n - 5) + 1)
                wait(act, tq_full, n + 1)
                act.activation(qst[0:KS, par, :, t * P:(t + 1) * P],
                               W_PS[0:KS, :].rearrange("p (h n) -> p h n", h=HG), ACT.Copy).then_inc(tq_ev, 1)

            def k_evac(n, par, t):
                wait(act, tk_full, n + 1)
                act.activation(kst[0:KS, par, :, t * P:(t + 1) * P],
                               W_PS[0:KS, :].rearrange("p (h n) -> p h n", h=HG), ACT.Copy).then_inc(tk_ev, 1)

            def exps(j, c, e):
                w, tile = ST_W[e], slice(ST_AT[e], ST_AT[e] + ST_W[e])
                bank = ST_PS[(NOP * c + e) % 2]
                n = NOP * j + e
                wait(act, st_full, n + 1)
                wait(act, pv_ok, n - NOP + 1)
                act.activation(pf[:, tile], bank[:, 0:w], ACT.Exp, scale=SCALE)
                act.activation(ph[:, tile], bank[:, 0:w], ACT.Exp, scale=SCALE).then_inc(p_ok, 1)

            def o_evac(j, i, h):
                wait(act, pv_ok, NOP * (j + 1))
                if h == 0:
                    wait(act, og_in, 16 * 2 * HG * i)
                    wait(act, d_in, 16 * i)
                act.activation(oraw[:, h, :], PV_PS[0:VW, :], ACT.Copy).then_inc(o_ev, 1)

            def o_high(i, g):
                wait(act, on_ok, i + 1)
                act.activation(on_h[:, g, :], on[:], ACT.Copy).then_inc(onh_ok, 1)

            def m_evac(i, par):
                wait(act, mt_full, i + 1)
                wait(act, m_in, 16 * i)
                act.activation(mrow[:], W_PS[0:(HG - 1) * TB, 0:P], ACT.Copy, scale=-1.0).then_inc(mt_ok, 1)

            def s_evac(b, t):
                n = 4 * b + t
                wait(act, wo_full, n + 1)
                wait(act, s_out[t % 2], 16 * (2 * b + t // 2 + 1))
                act.activation(s_sb[:, t % 2, :], W_PS[:], ACT.Copy).then_inc(s_ev, 1)

            def beat(r, c):
                j, k = 16 * r + c, c % 4
                attend, turned = there(j, NB), there(j + 5, NB)
                if c == 0 and isinstance(r, int) and r == 0:
                    act.wait_ge(w_lo, G + 1)

                d_s, t_s = at(c, 20)
                s_on = t_s is not None and there(r + d_s, B)

                def q_out():
                    if turned:
                        q_evac(j + 5, (c + 5) // 4 % 2, (c + 5) % 4)

                def o_out():
                    if there(j - 1, NB):
                        o_evac(j - 1, 4 * r + (c - 1) // 4, (c - 1) % 4)

                def xn_out():
                    d, t = at(c, 9)
                    if t is not None and there(r + 1 + d, B):
                        xt_high(r + 1 + d, t)

                if turned:
                    t_high(j + 5, (c + 5) % 2)
                xn_out()
                if attend:
                    exps(j, c, 0)
                if attend:
                    exps(j, c, 1)
                if k == 0 and (c - 8) // 4 % 4 != G - 1 and there(4 * r + (c - 8) // 4, B * G):
                    o_high(4 * r + (c - 8) // 4, (c - 8) // 4 % 4)
                if not s_on:
                    q_out()
                if isinstance(r, int) and r == 0 and -6 <= c <= -3:
                    split_w(c + 7)
                o_out()
                if attend:
                    exps(j, c, 2)
                if s_on:
                    s_evac(r + d_s, t_s)
                    q_out()
                if turned:
                    k_evac(j + 5, (c + 5) // 4 % 2, (c + 5) % 4)
                if k == 3 and there(j + 4, NB):
                    m_evac(4 * r + (c + 4) // 4, (c + 4) // 4 % 2)
                if there(j + 7, NB):
                    square(j + 7, (c + 7) % 2, (c + 7) // 4 % VR, (c + 7) % 4)
                if k == 3 and (c - 7) // 4 % 4 == G - 1 and there(4 * r + (c - 7) // 4, B * G):
                    o_high(4 * r + (c - 7) // 4, G - 1)

            act.sem_inc(s_out[0], 16)
            act.sem_inc(s_out[1], 16)
            split_w(0)
            run_beats(act, beat)
            act.wait_ge(c2_in, 48)

            def gate(b, m):
                n = MT * b + m
                wait(act, gu_full, n + 1)
                wait_slot(act, hf_ok, n, m)
                act.activation(gs[:, m % 2, :], GU_PS[2 * (m % 2)][:], ACT.Silu,
                               scale=sgu[:, 0, m:m + 1]).then_inc(gs_ok, 1)

            def high(b, m):
                n = MT * b + m
                wait(act, hf_ok, n + 1)
                if m == 0:
                    wait(act, dn_full, 4 * b)
                act.activation(ht_h[:, m, :], hf[:, m % 2, :], ACT.Copy).then_inc(hh_ok, 1)

            def outer(b, t):
                n = 4 * b + t
                wait(act, y_ok, n + 1)
                wait_slot(act, sgx_ok, n, t)
                act.activation(gt[:, t % 2, :], yt[:, t % 2, :], ACT.Silu).then_inc(g_ok, 1)

            def batch(b):
                for m in range(MT):
                    if isinstance(b, int) and 0 < m - O_PROJ <= TB:
                        s_evac(B - 1, m - O_PROJ - 1)
                    gate(b, m)
                    if m:
                        high(b, m - 1)
                    if isinstance(b, int):
                        if m == O_HIGH:
                            o_high(LAST, G - 1)
                high(b, MT - 1)
                for t in range(TB):
                    outer(b, t)

            batch(0)
            with act.Fori(1, B) as b:
                batch(b)

        @block.vector
        def _(dve):

            def split_w(g):
                dve.wait_ge(w_hi, g + 1)
                if g < G:
                    cols = slice(g * 3 * GC, (g + 1) * 3 * GC)
                    dve.tensor_tensor(wq_l[:, :, cols], stage[:, :, cols], wq_h[:, :, cols].bitcast(F32),
                                      ALU.subtract).then_inc(w_lo, 1)
                else:
                    dve.tensor_tensor(wo_l[:], stage[:, :, G * 3 * GC:], wo_h[:].bitcast(F32),
                                      ALU.subtract).then_inc(w_lo, 1)

            def ln_stats(b, t):
                n = 4 * b + t
                s = t % 2
                wait(dve, x_in[t], 16 * (b + 1))
                dve.bn_stats(st6[:, s, 0:6], xr[:, t, :]).then_inc(ln_s, 1)
                wait(dve, ln_s, n + 1)
                dve.tensor_copy(st6[:, s, 6:7], st6[:, s, 0:1])
                dve.bn_aggr(mv[:, s, 0:2], st6[:, s, 0:6]).then_inc(ln_a, 1)
                wait(dve, ln_a, n + 1)
                dve.tensor_scalar(ve[:, s, 0:1], mv[:, s, 1:2], LN_EPS, None, ALU.add).then_inc(ln_v, 1)

            def ln_apply(b, t):
                n = 4 * b + t
                s = t % 2
                wait(dve, ln_r, n + 1)
                dve.tensor_scalar(xr[:, t, :], xr[:, t, :], mv[:, s, 0:1], rstd[:, s, 0:1],
                                  ALU.subtract, ALU.mult).then_inc(xn_ok, 1)

            def xt_low(b, t):
                n = 4 * b + t
                wait(dve, xt_hi, n + 1)
                cols = slice(t * P, (t + 1) * P)
                dve.tensor_tensor(xnt_l[:, :, cols], W_PS[:].rearrange("p (k n) -> p k n", k=KT),
                                  xnt_h[:, :, cols].bitcast(F32), ALU.subtract).then_inc(xt_lo, 1)

            def squares(n, s):
                wait(dve, sq_ok, n + 1)
                wait(dve, rr_ok, n - 1)
                dve.tensor_reduce(ss[:, s, :], sq[:, s], AX.X, ALU.add).then_inc(ss_ok, 1)

            def unit_rms(n, s, v, t):
                wait(dve, rr_ok, n + 1)
                wait(dve, rope_ok, n - 1)
                wait(dve, vh_ok, n + 1)
                dve.tensor_tensor(qn[:, s].rearrange("p a h d -> p (a h) d"),
                                  QKV_PS[s][:, 0:2 * GC].rearrange("p (h d) -> p h d", d=HD),
                                  rr[:, s, :].rearrange("p (h o) -> p h o", o=1).to_broadcast([P, 2 * HG, HD]),
                                  ALU.mult).then_inc(qn_ok, 1)
                dve.tensor_tensor(va[:, v, t, :, HD:2 * HD],
                                  QKV_PS[s][:, 2 * GC:3 * GC].rearrange("p (h d) -> p h d", d=HD),
                                  va[:, v, t, :, 0:HD].bitcast(F32), ALU.subtract).then_inc(vl_ok, 1)

            def rope_sum(n, s):
                wait(dve, rope_ok, n + 1)
                wait(dve, tl_ok, n - 1)
                wait(dve, th_ok, n - 1)
                dve.tensor_tensor(qp[:, s, :], ra[:, 0].rearrange("p a h d -> p (a h d)"),
                                  rb[:, 0].rearrange("p a h d -> p (a h d)"), ALU.add).then_inc(qp_ok, 1)

            def t_low(n, s):
                wait(dve, th_ok, n + 1)
                dve.tensor_tensor(tt[:, s, :, 2:5:2, :], qp[:, s, :].rearrange("p (a h d) -> p h a d", a=2, h=HG),
                                  tt[:, s, :, 0:4:3, :].bitcast(F32), ALU.subtract).then_inc(tl_ok, 1)

            def p_low(j, e):
                tile = slice(ST_AT[e], ST_AT[e] + ST_W[e])
                wait(dve, p_ok, NOP * j + e + 1)
                dve.tensor_tensor(pl[:, tile], pf[:, tile], ph[:, tile].bitcast(F32),
                                  ALU.subtract).then_inc(pl_ok, 1)

            def maxima(r, c, ops):
                qb, w = c % 4, (c % 4 + 1) * P
                for o in ops:
                    if o >= len(SM_OPS[qb]):
                        continue
                    heads = SM_OPS[qb][o]
                    if qb == 0 and o == 0:
                        wait(dve, mt_full, 4 * r + c // 4)
                    wait(dve, sm_full, sm_count(r, c) + o + 1)
                    bank = X_PS[(sm_count(0, c) + o) % 2]
                    if heads == TURN:
                        wait(dve, m0_in, 16 * (4 * r + c // 4))
                        dve.tensor_scalar(mrow0[:], bank[0:TB, 0:P], -1.0, None, ALU.mult).then_inc(sm_ok, 1)
                        continue
                    h0 = heads[0]
                    dve.tensor_reduce(mx[:].rearrange("p (h t) -> p h t", t=TB)[:, h0:h0 + len(heads), qb],
                                      bank[:, 0:len(heads) * w].rearrange(
                                          "p (h n) -> p h n", n=w), AX.X, ALU.max).then_inc(sm_ok, 1)

            def recip(i):
                wait(dve, d_in, 16 * (i + 1))
                wait(dve, rd_out, 16 * i)
                dve.reciprocal(rd16[:], den16[:]).then_inc(rd_ok, 1)

            def o_low(i, g):
                wait(dve, onh_ok, i + 1)
                dve.tensor_tensor(on_l[:, g, :], on[:], on_h[:, g, :].bitcast(F32),
                                  ALU.subtract).then_inc(onl_ok, 1)

            def gu_weights(m):
                if m == 0:
                    wait(dve, qkv_full, NB)
                wait(dve, ws_in[m % 2], 16 * (m // 2 + 1))
                dve.tensor_scalar(wgu[:, m], xr[:, 2 * (m % 2):2 * (m % 2) + 2, :].bitcast(I32).rearrange(
                    "p a (k n) -> p (a k) n", n=2 * P), -ZERO, None, ALU.add).then_inc(wc_ok, 1)

            def beat(r, c):
                j, k = 16 * r + c, c % 4
                attend, mxs, rms = there(j, NB), there(j + 4, NB), there(j + 6, NB)
                if rms:
                    squares(j + 6, (c + 6) % 2)
                if there(j + 5, NB):
                    t_low(j + 5, (c + 5) % 2)
                if mxs:
                    maxima(r, c + 4, SM_A[k])
                if mxs:
                    maxima(r, c + 4, SM_T[k])
                d, t = at(c, 9)
                if t is not None and there(r + 1 + d, B):
                    xt_low(r + 1 + d, t)
                if attend:
                    p_low(j, 0)
                if rms:
                    unit_rms(j + 6, (c + 6) % 2, (c + 6) // 4 % VR, (c + 6) % 4)
                if mxs:
                    maxima(r, c + 4, SM_B[k])
                if isinstance(r, int) and r == 0 and c == -8:
                    dve.wait_ge(id_in, 16)
                    dve.tensor_copy(idr[:], idf[:]).then_inc(idr_ok, 1)
                if k == 0 and (c - 8) // 4 % 4 == G - 1 and there(4 * r + (c - 8) // 4, B * G):
                    o_low(4 * r + (c - 8) // 4, (c - 8) // 4 % 4)
                if attend:
                    p_low(j, 1)
                if k == 0 and (c - 8) // 4 % 4 != G - 1 and there(4 * r + (c - 8) // 4, B * G):
                    o_low(4 * r + (c - 8) // 4, (c - 8) // 4 % 4)
                if k == 1 and there(4 * r + (c - 5) // 4, B * G):
                    recip(4 * r + (c - 5) // 4)
                if mxs:
                    maxima(r, c + 4, SM_C[k])
                if isinstance(r, int) and r == B - 1 and 0 <= c - 10 < EARLY:
                    gu_weights(c - 10)
                b, t = ln_at(r, c)
                if t is not None:
                    ln_stats(b, t)
                if rms:
                    rope_sum(j + 6, (c + 6) % 2)
                if attend:
                    p_low(j, 2)
                if t is not None:
                    ln_apply(b, t)
                if isinstance(r, int) and r == 0 and c in SPLIT_AT:
                    split_w(SPLIT_AT.index(c))

            run_beats(dve, beat)

            def hidden(b, m):
                n = MT * b + m
                wait(dve, gs_ok, n + 1)
                wait_slot(dve, hh_ok, n, m)
                wait_slot(dve, hl_ok, n, m)
                dve.scalar_tensor_tensor(hf[:, m % 2, :], GU_PS[2 * (m % 2) + 1][:], sgu[:, 1, m:m + 1],
                                         gs[:, m % 2, :], ALU.mult, ALU.mult).then_inc(hf_ok, 1)

            def low(b, m):
                wait(dve, hh_ok, MT * b + m + 1)
                dve.tensor_tensor(ht_l[:, m, :], hf[:, m % 2, :], ht_h[:, m, :].bitcast(F32),
                                  ALU.subtract).then_inc(hl_ok, 1)

            def scaled(b, t):
                n = 4 * b + t
                wait(dve, dn_full, n + 1)
                wait_slot(dve, g_ok, n, t)
                dve.tensor_tensor(yt[:, t % 2, :], DN_PS[t][:], sdb[:], ALU.mult).then_inc(y_ok, 1)

            def finish(b, t):
                n = 4 * b + t
                s = t % 2
                wait(dve, g_ok, n + 1)
                wait(dve, xs_in[t], 32 * (b + 1))
                wait(dve, r_out[s], 16 * (2 * b + t // 2))
                dve.tensor_tensor(res[:, s, :], gt[:, s, :], xs[:, t, 1, :], ALU.mult).then_inc(sgx_ok, 1)
                wait(dve, sgx_ok, n + 1)
                dve.tensor_tensor(res[:, s, :], res[:, s, :], xs[:, t, 0, :], ALU.add).then_inc(res_ok, 1)

            def batch(b):
                for m in range(MT):
                    hidden(b, m)
                    if m:
                        low(b, m - 1)
                    if isinstance(b, int):
                        if m == 0:
                            recip(LAST)
                        if m >= 2 and EARLY + m - 2 < MT:
                            gu_weights(EARLY + m - 2)
                        if m == O_HIGH:
                            o_low(LAST, G - 1)
                low(b, MT - 1)
                for t in range(TB):
                    scaled(b, t)
                    if t:
                        finish(b, t - 1)
                finish(b, TB - 1)

            dve.wait_ge(c2_in, 48)
            batch(0)
            with dve.Fori(1, B) as b:
                batch(b)

        @block.tensor
        def _(pe):
            pe.wait_ge(id_in, 16)

            def xn_turn(n_, b, t):
                n = 4 * b + t
                wait(pe, xn_ok, n + 1)
                wait(pe, xt_lo, n)
                wait(pe, tk_ev, n_ + 1)
                for k in range(KT):
                    op = pe.transpose(W_PS[:, k * P:(k + 1) * P], xr[:, t, k * P:(k + 1) * P], idf[:])
                op.then_inc(xt_full, 1)

            def project(r, c, half_):
                n, g, t, s = 16 * r + c, c // 4 % 4, c % 4, c % 2
                if half_ == 0:
                    if g == 0:
                        b = r + c // 16
                        wait(pe, xt_hi, 4 * b + t + 1)
                        wait(pe, xt_lo, 4 * b + t + 1)
                    if isinstance(n, int) and n < 16:
                        pe.wait_ge(w_lo, g + 1)
                    wait(pe, sq_ok, n - 1)
                    wait(pe, vh_ok, n - 1)
                    wait(pe, vl_ok, n - 1)
                cols = slice(g * 3 * GC, (g + 1) * 3 * GC)
                todo = [(x_, w_, k) for x_, w_ in ((xnt_h, wq_h), (xnt_l, wq_h), (xnt_h, wq_l)) for k in range(KT)]
                m = len(todo) // 2
                for a, (x_, w_, k) in list(enumerate(todo))[half_ * m:half_ * m + m]:
                    op = pe.matmul(QKV_PS[s][:, 0:3 * GC], x_[:, k, t * P:(t + 1) * P], w_[:, k, cols],
                                   start=(a == 0), stop=(a == len(todo) - 1))
                if half_:
                    op.then_inc(qkv_full, 1)

            def turn(r, c, a):
                n, s = 16 * r + c, c % 2
                wait(pe, tl_ok, n + 1)
                wait(pe, tq_ev if a else tk_ev, n + a)
                for h in range(HG):
                    op = pe.transpose(W_PS[0:KS, h * P:(h + 1) * P].bitcast(F32R),
                                      tt[:, s, h, 3 * a:3 * a + 3, :].rearrange("p c d -> p (c d)"), idr[:])
                op.then_inc((tq_full, tk_full)[a], 1)

            def scores_t(r, c, e):
                n, par, h = NOP * (16 * r + c) + e, c // 4 % 2, c % 4
                if h < 2 and e == 0:
                    wait(pe, m_in if h else m0_in, 16 * (4 * r + c // 4 + 1))
                wait(pe, p_ok, n - 1)
                bank = ST_PS[(NOP * c + e) % 2]
                for j, c0, w in ST_OPS[e]:
                    pe.matmul(bank[:, c0:c0 + w], kst[0:KS + 1, par, h, j * P:(j + 1) * P],
                              qst[0:KS + 1, par, h, j * P:N], start=True, stop=False)
                    op = pe.matmul(bank[:, c0:c0 + P], idb[:], msk_t[:], start=False, stop=True)
                op.then_inc(st_full, 1)

            def p_v(r, c, e):
                j_, v, h = 16 * r + c, c // 4 % VR, c % 4
                wait(pe, pl_ok, NOP * j_ + e + 1)
                if e == 0:
                    wait(pe, o_ev, j_)
                    if h == 0:
                        wait(pe, vl_ok, j_ + 4)
                for j, c0, w in ST_OPS[e]:
                    a = ST_AT[e] + c0
                    for part in (ph, pl):
                        op = pe.matmul(PV_PS[0:VW, j * P:N], va[:, v, j, h, :], part[:, a:a + w],
                                       start=(j == 0 and part is ph), stop=(j == 2 and part is pl))
                op.then_inc(pv_ok, 1)

            def maxima(r, c, ops):
                n, par, qb, w = 16 * r + c, c // 4 % 2, c % 4, (c % 4 + 1) * P
                for o in ops:
                    if o >= len(SM_OPS[qb]):
                        continue
                    if o == 0:
                        wait(pe, tq_ev, n + 1)
                        wait(pe, tk_ev, n + 1)
                    wait(pe, sm_ok, sm_count(r, c) + o - 1)
                    bank = X_PS[(sm_count(0, c) + o) % 2]
                    if SM_OPS[qb][o] == TURN:
                        wait(pe, sm_ok, sm_count(r, c) + 1)
                        pe.transpose(bank[0:TB, 0:P], mx[:, 0:TB], idf[:]).then_inc(sm_full, 1)
                        continue
                    for a, h in enumerate(SM_OPS[qb][o]):
                        pe.matmul(bank[:, a * w:(a + 1) * w], qst[0:KS, par, h, qb * P:(qb + 1) * P],
                                  kst[0:KS, par, h, 0:w], start=True, stop=False)
                        op = pe.matmul(bank[:, (a + 1) * w - P:(a + 1) * w], idb[:], msk_s[:], start=False, stop=True)
                    op.then_inc(sm_full, 1)

            def max_turn(r, c):
                wait(pe, sm_ok, sm_count(r, c + 1))
                wait(pe, tk_ev, min(16 * r + c + 2, NB) if isinstance(r, int) else 16 * r + c + 2)
                pe.transpose(W_PS[0:(HG - 1) * TB, 0:P], mx[:, TB:], idf[:]).then_inc(mt_full, 1)

            def out_proj(b, t, part):
                if t == 0 and part != 1:
                    wait(pe, onl_ok if part else onh_ok, 4 * b + 4)
                todo = [(o_, w_, g) for o_, w_ in ((on_h, wo_h), (on_h, wo_l), (on_l, wo_h)) for g in range(G)]
                m = len(todo) // 3
                for a, (o_, w_, g) in list(enumerate(todo))[part * m:part * m + m]:
                    op = pe.matmul(W_PS[:], o_[:, g, t * P:(t + 1) * P], w_[:, g, :],
                                   start=(a == 0), stop=(a == len(todo) - 1))
                if part == 2:
                    op.then_inc(wo_full, 1)

            def beat(r, c):
                j, k = 16 * r + c, c % 4
                if isinstance(r, int) and r == 0 and c == -6:
                    pe.wait_ge(idr_ok, 1)
                if isinstance(r, int) and r == 0 and c == -4:
                    pe.wait_ge(c_in, 16 * 7)
                    pe.wait_ge(ones_ok, 4)
                attend, mxs, proj = there(j, NB), there(j + 4, NB), there(j + 7, NB)
                turned, before = there(j + 5, NB), there(j - 1, NB)
                d_o, t_o = at(c, 20)
                d_x, t_x = at(c, 9)
                early = isinstance(r, int) and r == 0 and c < 0

                def turn_q():
                    if turned:
                        w_free()
                        if t_o is not None and there(r + d_o, B):
                            wait(pe, s_ev, 4 * (r + d_o) + t_o + 1)
                        if t_x is not None and there(r + 1 + d_x, B):
                            wait(pe, xt_lo, 4 * (r + 1 + d_x) + t_x + 1)
                        turn(r, c + 5, 0)

                def turn_k():
                    if turned:
                        turn(r, c + 5, 1)

                def w_bank(part):
                    if t_o is not None and there(r + d_o, B):
                        if part == 0:
                            w_free()
                            wait(pe, tk_ev, min(j + 5, NB) if isinstance(j, int) else j + 5)
                        out_proj(r + d_o, t_o, part)
                    if part == 0 and early and t_x is not None and there(r + 1 + d_x, B):
                        xn_turn(j + 4, r + 1 + d_x, t_x)

                def w_free():
                    if k == 0 and attend:
                        wait(pe, mt_ok, 4 * r + c // 4 + 1)

                def banks(group):
                    if mxs:
                        maxima(r, c + 4, group[k])

                if attend:
                    scores_t(r, c, 0)
                if not early and t_x is not None and there(r + 1 + d_x, B):
                    w_free()
                    xn_turn(j + 4, r + 1 + d_x, t_x)
                if attend:
                    scores_t(r, c, 1)
                banks(SM_A)
                w_bank(0)
                if before:
                    p_v(r, c - 1, 1)
                    p_v(r, c - 1, 2)
                banks(SM_T)
                if t_o is not None or t_x is not None:
                    banks(SM_B)
                w_bank(1)
                if t_o is not None:
                    if attend:
                        scores_t(r, c, 2)
                    w_bank(2)
                    if proj:
                        project(r, c + 7, 0)
                turn_q()
                if t_o is None and t_x is None:
                    banks(SM_B)
                if t_o is None:
                    if attend:
                        scores_t(r, c, 2)
                    if proj:
                        project(r, c + 7, 0)
                banks(SM_C)
                if t_o is None:
                    turn_k()
                if proj:
                    project(r, c + 7, 1)
                if t_o is not None:
                    turn_k()
                if k == 3 and mxs:
                    max_turn(r, c + 4)
                if attend:
                    p_v(r, c, 0)
            run_beats(pe, beat)

            def gate_up(b, m):
                n = MT * b + m
                wait_slot(pe, hf_ok, n, m)
                for a in range(2):
                    todo = [(x_, k) for x_ in (xnt_h, xnt_l) for k in range(KT)]
                    for j, (x_, k) in enumerate(todo):
                        op = pe.matmul(GU_PS[2 * (m % 2) + a][:], wgu[:, m, k, a * P:(a + 1) * P], x_[:, k, :],
                                       start=(j == 0), stop=(j == len(todo) - 1))
                op.then_inc(gu_full, 1)

            def down(b, t):
                n = 4 * b + t
                wait_slot(pe, y_ok, n, t, TB)
                for m in range(MT):
                    if t == 0:
                        wait(pe, hl_ok, MT * b + m + 1)
                    for h_ in (ht_h, ht_l):
                        op = pe.matmul(DN_PS[t][:], h_[:, m, t * P:(t + 1) * P], wd[:, m, :],
                                       start=(m == 0 and h_ is ht_h), stop=(m == MT - 1 and h_ is ht_l))
                op.then_inc(dn_full, 1)

            def batch(b):
                wait(pe, xb_in, 32 * (b + 1))
                for m in range(MT):
                    if isinstance(b, int):
                        wait(pe, wc_ok, m + 1)
                    gate_up(b, m)
                    if isinstance(b, int) and 0 <= m - O_PROJ < TB:
                        wait(pe, s_ev, 4 * (B - 1) + m - O_PROJ)
                        for part in range(3):
                            out_proj(B - 1, m - O_PROJ, part)
                if isinstance(b, int):
                    pe.wait_ge(s_ev, 4 * B)
                    pe.wait_ge(o_ev, NB)
                    pe.wait_ge(wd_ok, MT)
                for t in range(TB):
                    down(b, t)

            pe.wait_ge(sm_ok, SM_UNIT * B * G)
            pe.wait_ge(vl_ok, NB)
            batch(0)
            with pe.Fori(1, B) as b:
                batch(b)


def kernel(L0_attn_x, L0_attn_w_qkv, L0_attn_w_out, L0_attn_q_gamma, L0_attn_k_gamma,
           L0_ffn_wq_gate, L0_ffn_s_gate, L0_ffn_wq_up, L0_ffn_s_up, L0_ffn_wq_down, L0_ffn_s_down):
    import ml_dtypes
    import concourse.bacc as bacc
    from concourse.bass_utils import run_bass_kernel_spmd

    def ar(a):
        return np.asarray(a)

    inv = (1.0 / np.float32(THETA) ** (np.arange(0, HD, 2, dtype=np.float32) / np.float32(HD))).astype(np.float32)
    ang = np.arange(N, dtype=np.float32)[:, None] * inv[None, :]
    ang = np.concatenate([ang, ang], -1)
    sign = np.where(np.arange(HD) < HD // 2, -1.0, 1.0)
    root = np.sqrt(float(HD))
    cos_tab = (np.cos(ang.astype(np.float64)) * root).astype(np.float32)
    sin_tab = (np.sin(ang.astype(np.float64)) * sign * root).astype(np.float32)
    tri = np.arange(P)
    arrays = {
        "x": np.ascontiguousarray(ar(L0_attn_x)),
        "w_qkv": np.ascontiguousarray(ar(L0_attn_w_qkv).reshape(KT, P, 3, G, GC).transpose(1, 0, 3, 2, 4)
                                      .reshape(P, KT, G * 3 * GC)),
        "w_out": np.ascontiguousarray(ar(L0_attn_w_out).reshape(KT, P, H).transpose(1, 0, 2)),
        "q_gamma": ar(L0_attn_q_gamma).reshape(1, HD),
        "k_gamma": ar(L0_attn_k_gamma).reshape(1, HD),
        "w_gu": np.ascontiguousarray(np.stack([ar(w).reshape(MT, P, KT, P).transpose(0, 3, 2, 1)
                                               for w in (L0_ffn_wq_gate, L0_ffn_wq_up)], 3).reshape(MT, P, KT, 2 * P)),
        "s_gate": np.ascontiguousarray(ar(L0_ffn_s_gate).reshape(MT, P).T),
        "s_up": np.ascontiguousarray(ar(L0_ffn_s_up).reshape(MT, P).T),
        "w_down": np.ascontiguousarray(ar(L0_ffn_wq_down).T.reshape(MT, P, H)),
        "s_down": ar(L0_ffn_s_down).reshape(1, H),
        "cos_tab": np.ascontiguousarray(cos_tab.reshape(TB, P, HD).transpose(1, 0, 2)),
        "sin_tab": np.ascontiguousarray(sin_tab.reshape(TB, P, HD).transpose(1, 0, 2)),
        "ident": np.eye(P, dtype=np.float32),
        "ident_b": np.eye(P, dtype=np.float32).astype(ml_dtypes.bfloat16),
        "mask_s": np.where(tri[None, :] > tri[:, None], NEG, 0.0).astype(ml_dtypes.bfloat16),
        "mask_t": np.where(tri[:, None] > tri[None, :], NEG, 0.0).astype(ml_dtypes.bfloat16),
    }
    nc = bacc.Bacc("TRN2", target_bir_lowering=False, num_devices=1)
    d = {k: nc.dram_tensor(k, a.shape, mybir.dt.from_np(a.dtype), kind="ExternalInput").ap()
         for k, a in arrays.items()}
    s_dram = nc.dram_tensor("s_dram", (B, N, H), F32, kind="Internal").ap()
    rd_dram = nc.dram_tensor("rd_dram", (1, HG * N), F32, kind="Internal").ap()
    xnt_dram = nc.dram_tensor("xnt_dram", (2, B, P, KT, N), F32, kind="Internal").ap()
    out = nc.dram_tensor("out", (B, N, H), F32, kind="ExternalOutput").ap()
    build(nc, d["x"], d["w_qkv"], d["w_out"], d["q_gamma"], d["k_gamma"], d["w_gu"], d["s_gate"], None,
          d["s_up"], d["w_down"], d["s_down"], d["cos_tab"], d["sin_tab"], d["ident"], d["ident_b"],
          d["mask_s"], d["mask_t"], s_dram, rd_dram, xnt_dram, out)
    r = run_bass_kernel_spmd(nc, [arrays], core_ids=[0])
    return r.results[0]["out"]
```
